# Optimizing a Trainium2 kernel written in Bass

```python
import numpy as np
import jax
import jax.numpy as jnp

def _softmax(x, axis=-1):
    return jax.nn.softmax(x, axis=axis)

def _gelu(x):
    return jax.nn.gelu(x, approximate=True)

def _silu(x):
    return jax.nn.silu(x)

def _sigmoid(x):
    return jax.nn.sigmoid(x)

def _layernorm(x, axis=-1, eps=1e-05):
    m = jnp.mean(x, axis=axis, keepdims=True)
    v = jnp.var(x, axis=axis, keepdims=True)
    return (x - m) / jnp.sqrt(v + eps)

def _scatter_add(tgt, idx, src, axis=0):
    return tgt.at[idx].add(src)

def _segment_sum(src, seg, n):
    return jax.ops.segment_sum(src, seg, n)
kernel_name = 'mk_flamingo_gated_d1_seqx_r8_d154a9'

def setup_inputs(seed: int=0):
    np.random.seed(seed)
    _w = jnp.asarray

    def _rec_inputs():
        import jax
        import jax.numpy as jnp
        _rk = jax.random.key(seed)
        x = 7.22e-05 + 1 * jax.random.normal(jax.random.fold_in(_rk, 1), (8, 128, 512), jnp.float32)
        _lenS = 128 - jax.random.randint(jax.random.fold_in(_rk, 7), (8,), 0, max(1, 128 // 4) + 1, jnp.int32)
        _lenS2 = 128 - jax.random.randint(jax.random.fold_in(_rk, 8), (8,), 0, max(1, 128 // 4) + 1, jnp.int32)
        _ctx_4096P = jax.random.normal(jax.random.fold_in(_rk, 11), (8, 16, 512), jnp.float32)
        _ctx_4096c = jax.random.dirichlet(jax.random.fold_in(_rk, 511), 0.3 * jnp.ones((16,), jnp.float32), (8, 128))
        _ctx_4096t = jnp.einsum('bsk,bkd->bsd', _ctx_4096c, _ctx_4096P)
        _ctx_4096t = _ctx_4096t * jax.lax.rsqrt(jnp.mean(jnp.square(_ctx_4096t)) + 1e-12) * 0.953939
        ctx_4096 = 4.13588e-05 + 0.999923 * (_ctx_4096t + 0.3 * jax.random.normal(jax.random.fold_in(_rk, 611), (8, 128, 512), jnp.float32))
        _validS = jnp.arange(128)[None, :] < _lenS[:, None]
        _validS2 = jnp.arange(128)[None, :] < _lenS2[:, None]
        _causal = jnp.tril(jnp.ones((128, 128), dtype=bool))
        mask_1x1xSxS2_bk0 = jnp.logical_not(jnp.broadcast_to(_validS2[0:1, None, None, :], (1, 1, 128, 128)))
        _g = jax.random.normal(jax.random.fold_in(_rk, 9001), (2, 1), jnp.float32)
        _g = jnp.sign(_g) * jnp.maximum(jnp.abs(_g), 1.0) + (_g == 0) * 1.0
        g_xattn = _g[0]
        g_ffn = _g[1]
        return (x, ctx_4096, mask_1x1xSxS2_bk0, g_xattn, g_ffn)
    x, ctx_4096, mask_1x1xSxS2_bk0, g_xattn, g_ffn = _rec_inputs()

    def _L0_xattn_setup():
        import jax, jax.numpy as jnp
        import numpy as np
        B, T, D_MODEL = (1, 256, 512)
        NUM_Q_HEADS, NUM_KV_HEADS, KEY_SIZE = (32, 8, 128)
        ATTN_MULT = 0.08838834764831845
        MAX_ATTN_VAL = 30.0

        def rotate_half(x):
            x1, x2 = jnp.split(x, 2, axis=-1)
            return jnp.concatenate((-x2, x1), axis=-1)

        def apply_rope(x):
            b, t, h, d = x.shape
            exponents = jnp.arange(0, d, 2, dtype=jnp.float32)
            inv_freq = 1.0 / 10000.0 ** (exponents / d)
            pos = jnp.arange(t, dtype=jnp.float32)
            phase = pos[:, None] * inv_freq[None, :]
            phase = jnp.tile(phase, (1, 2))[None, :, None, :]
            return (x * jnp.cos(phase) + rotate_half(x) * jnp.sin(phase)).astype(x.dtype)
        key = jax.random.key(seed)
        ks = jax.random.split(key, 8)
        query = jax.random.normal(ks[0], (B, T, D_MODEL), dtype=jnp.float32)
        kk = jax.random.normal(ks[1], (B, T, D_MODEL), dtype=jnp.float32)
        vv = jax.random.normal(ks[2], (B, T, D_MODEL), dtype=jnp.float32)
        mask = jnp.tril(jnp.ones((T, T), dtype=bool))[None, None, :, :]
        s = 0.02
        Wq = jax.random.normal(ks[3], (D_MODEL, NUM_Q_HEADS * KEY_SIZE), dtype=jnp.float32) * s
        Wk = jax.random.normal(ks[4], (D_MODEL, NUM_KV_HEADS * KEY_SIZE), dtype=jnp.float32) * s
        Wv = jax.random.normal(ks[5], (D_MODEL, NUM_KV_HEADS * KEY_SIZE), dtype=jnp.float32) * s
        Wo = jax.random.normal(ks[6], (NUM_Q_HEADS * KEY_SIZE, D_MODEL), dtype=jnp.float32) * s
        return {'query': query, 'key': kk, 'value': vv, 'mask': mask, 'Wq': Wq, 'Wk': Wk, 'Wv': Wv, 'Wo': Wo}
    _L0_xattn_all = _L0_xattn_setup()
    _L0_xattn_in = {k: v for k, v in _L0_xattn_all.items() if k in ('Wq', 'Wk', 'Wv', 'Wo')}
    del _L0_xattn_all

    def _L0_ffn_setup():
        import jax, jax.numpy as jnp
        import numpy as np
        HIDDEN = 512
        INTER = 1376
        GROUPSIZE = 128
        PACK = 8

        def dequant_gptq(qweight, scales, zeros, groupsize):
            K = qweight.shape[0] * PACK
            N = qweight.shape[1]
            k = jnp.arange(K)
            q = qweight[k // PACK, :] >> (k % PACK * 4)[:, None] & 15
            n = jnp.arange(N)
            z = zeros[:, n // PACK] >> (n % PACK * 4)[None, :] & 15
            s = scales.astype(jnp.float32)
            zp = (z.astype(jnp.float32) + 1.0) * s
            g = k // groupsize
            return q.astype(jnp.float32) * s[g] - zp[g]
        key = jax.random.key(seed)
        ks = jax.random.split(key, 11)
        imax = 2147483647
        G_h = HIDDEN // GROUPSIZE
        G_i = (INTER + GROUPSIZE - 1) // GROUPSIZE
        x = (jax.random.normal(ks[0], (2, 256, HIDDEN), dtype=jnp.float32) * 0.5).astype(jnp.float16)
        return {'x': x, 'gate_qweight': jax.random.randint(ks[1], (HIDDEN // PACK, INTER), 0, imax, dtype=jnp.int32), 'gate_scales': (jax.random.uniform(ks[2], (G_h, INTER), dtype=jnp.float32) * 0.01 + 0.001).astype(jnp.float16), 'gate_zeros': jax.random.randint(ks[3], (G_h, INTER // PACK), 0, imax, dtype=jnp.int32), 'up_qweight': jax.random.randint(ks[4], (HIDDEN // PACK, INTER), 0, imax, dtype=jnp.int32), 'up_scales': (jax.random.uniform(ks[5], (G_h, INTER), dtype=jnp.float32) * 0.01 + 0.001).astype(jnp.float16), 'up_zeros': jax.random.randint(ks[6], (G_h, INTER // PACK), 0, imax, dtype=jnp.int32), 'down_qweight': jax.random.randint(ks[7], (INTER // PACK, HIDDEN), 0, imax, dtype=jnp.int32), 'down_scales': (jax.random.uniform(ks[8], (G_i, HIDDEN), dtype=jnp.float32) * 0.01 + 0.001).astype(jnp.float16), 'down_zeros': jax.random.randint(ks[9], (G_i, HIDDEN // PACK), 0, imax, dtype=jnp.int32)}
    _L0_ffn_all = _L0_ffn_setup()
    _L0_ffn_in = {k: v for k, v in _L0_ffn_all.items() if k in ('gate_qweight', 'gate_scales', 'gate_zeros', 'up_qweight', 'up_scales', 'up_zeros', 'down_qweight', 'down_scales', 'down_zeros')}
    del _L0_ffn_all
    return {'x': x, 'ctx_4096': ctx_4096, 'mask_1x1xSxS2_bk0': mask_1x1xSxS2_bk0, 'g_xattn': g_xattn, 'g_ffn': g_ffn, 'L0_xattn_Wq': _L0_xattn_in['Wq'], 'L0_xattn_Wk': _L0_xattn_in['Wk'], 'L0_xattn_Wv': _L0_xattn_in['Wv'], 'L0_xattn_Wo': _L0_xattn_in['Wo'], 'L0_ffn_gate_qweight': _L0_ffn_in['gate_qweight'], 'L0_ffn_gate_scales': _L0_ffn_in['gate_scales'], 'L0_ffn_gate_zeros': _L0_ffn_in['gate_zeros'], 'L0_ffn_up_qweight': _L0_ffn_in['up_qweight'], 'L0_ffn_up_scales': _L0_ffn_in['up_scales'], 'L0_ffn_up_zeros': _L0_ffn_in['up_zeros'], 'L0_ffn_down_qweight': _L0_ffn_in['down_qweight'], 'L0_ffn_down_scales': _L0_ffn_in['down_scales'], 'L0_ffn_down_zeros': _L0_ffn_in['down_zeros']}

def reference(x, ctx_4096, mask_1x1xSxS2_bk0, g_xattn, g_ffn, L0_xattn_Wq, L0_xattn_Wk, L0_xattn_Wv, L0_xattn_Wo, L0_ffn_gate_qweight, L0_ffn_gate_scales, L0_ffn_gate_zeros, L0_ffn_up_qweight, L0_ffn_up_scales, L0_ffn_up_zeros, L0_ffn_down_qweight, L0_ffn_down_scales, L0_ffn_down_zeros):
    import jax
    import jax.numpy as jnp

    def _L0_xattn_ref(query, key, value, mask, Wq, Wk, Wv, Wo):
        import jax, jax.numpy as jnp
        import numpy as np
        B, T, D_MODEL = (1, 256, 512)
        NUM_Q_HEADS, NUM_KV_HEADS, KEY_SIZE = (32, 8, 128)
        ATTN_MULT = 0.08838834764831845
        MAX_ATTN_VAL = 30.0

        def rotate_half(x):
            x1, x2 = jnp.split(x, 2, axis=-1)
            return jnp.concatenate((-x2, x1), axis=-1)

        def apply_rope(x):
            b, t, h, d = x.shape
            exponents = jnp.arange(0, d, 2, dtype=jnp.float32)
            inv_freq = 1.0 / 10000.0 ** (exponents / d)
            pos = jnp.arange(t, dtype=jnp.float32)
            phase = pos[:, None] * inv_freq[None, :]
            phase = jnp.tile(phase, (1, 2))[None, :, None, :]
            return (x * jnp.cos(phase) + rotate_half(x) * jnp.sin(phase)).astype(x.dtype)
        b, t, _ = query.shape
        d = KEY_SIZE
        h, kv_h = (NUM_Q_HEADS, NUM_KV_HEADS)
        g = h // kv_h
        q = (query @ Wq).reshape(b, t, h, d)
        k = (key @ Wk).reshape(b, t, kv_h, d)
        v = (value @ Wv).reshape(b, t, kv_h, d)
        q = apply_rope(q)
        k = apply_rope(k)
        q = q.reshape(b, t, kv_h, g, d)
        logits = jnp.einsum('btkgd,bTkd->bkgtT', q, k).astype(jnp.float32)
        logits = logits * ATTN_MULT
        logits = MAX_ATTN_VAL * jnp.tanh(logits / MAX_ATTN_VAL)
        m = mask[:, :, None, :, :]
        logits = jnp.where(m, logits, -1e+30)
        weights = jax.nn.softmax(logits, axis=-1).astype(query.dtype)
        attn = jnp.einsum('bkgtT,bTkd->btkgd', weights, v)
        attn = attn.reshape(b, t, h * d)
        return attn @ Wo

    def _L0_ffn_ref(x, gate_qweight, gate_scales, gate_zeros, up_qweight, up_scales, up_zeros, down_qweight, down_scales, down_zeros):
        import jax, jax.numpy as jnp
        import numpy as np
        HIDDEN = 512
        INTER = 1376
        GROUPSIZE = 128
        PACK = 8

        def dequant_gptq(qweight, scales, zeros, groupsize):
            K = qweight.shape[0] * PACK
            N = qweight.shape[1]
            k = jnp.arange(K)
            q = qweight[k // PACK, :] >> (k % PACK * 4)[:, None] & 15
            n = jnp.arange(N)
            z = zeros[:, n // PACK] >> (n % PACK * 4)[None, :] & 15
            s = scales.astype(jnp.float32)
            zp = (z.astype(jnp.float32) + 1.0) * s
            g = k // groupsize
            return q.astype(jnp.float32) * s[g] - zp[g]
        B, S, H = x.shape
        x2 = x.reshape(-1, H).astype(jnp.float32)
        Wg = dequant_gptq(gate_qweight, gate_scales, gate_zeros, GROUPSIZE)
        Wu = dequant_gptq(up_qweight, up_scales, up_zeros, GROUPSIZE)
        Wd = dequant_gptq(down_qweight, down_scales, down_zeros, GROUPSIZE)
        gate = x2 @ Wg
        up = x2 @ Wu
        inter = gate * jax.nn.sigmoid(gate) * up
        out = (inter @ Wd).astype(jnp.float16)
        return out.reshape(B, S, H)
    x = x + jnp.tanh(g_xattn[0]) * _L0_xattn_ref(_layernorm(x, axis=-1), ctx_4096, ctx_4096, mask_1x1xSxS2_bk0, L0_xattn_Wq, L0_xattn_Wk, L0_xattn_Wv, L0_xattn_Wo)
    x = x + jnp.tanh(g_ffn[0]) * _L0_ffn_ref(_layernorm(x, axis=-1), L0_ffn_gate_qweight, L0_ffn_gate_scales, L0_ffn_gate_zeros, L0_ffn_up_qweight, L0_ffn_up_scales, L0_ffn_up_zeros, L0_ffn_down_qweight, L0_ffn_down_scales, L0_ffn_down_zeros)
    return x

_drawn_inputs = setup_inputs


def setup_inputs(seed=0):
    import zlib

    import numpy as np

    out = dict(_drawn_inputs(seed))
    spreads = {}
    factors = {}
    for name, (base, spread) in spreads.items():
        noise = np.random.default_rng([zlib.crc32(name.encode()), seed]).standard_normal(out[name].shape)
        drawn = base * np.exp(spread * noise) if base else spread * noise
        out[name] = jnp.asarray(drawn.astype(out[name].dtype))
    for name, factor in factors.items():
        out[name] = (out[name] * factor).astype(out[name].dtype)
    return out
```

```python
from contextlib import ExitStack

import numpy as np

import concourse.bass as bass
from concourse import mybir

ALU = mybir.AluOpType
ACT = mybir.ActivationFunctionType
F32 = mybir.dt.float32
F32R = mybir.dt.float32r
F16 = mybir.dt.float16
U32 = mybir.dt.uint32
U8 = mybir.dt.uint8
AX_X = mybir.AxisListType.X

P = 128
B = 8
T = 128
C = 512
KT = C // P
KV = 8
HG = 4
D = 128
GC = HG * D
SLOTS = KV * B
LOOPED = 16
INTER = 1376
NT = 11
LAST = INTER - (NT - 1) * P
PACK = 8
WORDS = C // PACK
HALF = B // 2
ATTN_MULT = 0.08838834764831845
MAX_ATTN = 30.0
EPS = 1e-5


def wait(eng, s, n):
    if not isinstance(n, int) or n > 0:
        eng.wait_ge(s, n)


def split_matmul(nc, out, w_hi, w_lo, m_hi, m_lo, first, last):
    nc.tensor.matmul(out, w_hi, m_hi, start=first, stop=False)
    nc.tensor.matmul(out, w_hi, m_lo, start=False, stop=False)
    return nc.tensor.matmul(out, w_lo, m_hi, start=False, stop=last)


def flamingo_block(nc, x, ctx_in, mask, g_xattn, g_ffn, Wq, Wk, Wv, Wo,
                   gate_q, gate_s, gate_z, up_q, up_s, up_z, down_q, down_s, down_z,
                   cos_sin, nibble, out):
    with ExitStack() as whole:
        acc = whole.enter_context(nc.sbuf_tensor("acc", [P, B, C], F32))
        xT_hi = whole.enter_context(nc.sbuf_tensor("xT_hi", [P, B, KT, T], F32R))
        xT_lo = whole.enter_context(nc.sbuf_tensor("xT_lo", [P, B, KT, T], F32R))
        xn = whole.enter_context(nc.sbuf_tensor("xn", [P, 2, C], F32))
        stats = whole.enter_context(nc.sbuf_tensor("stats", [P, B, 6], F32))
        moments = whole.enter_context(nc.sbuf_tensor("moments", [P, B, 2], F32))
        rstd = whole.enter_context(nc.sbuf_tensor("rstd", [P, B, 1], F32))
        minus_half = whole.enter_context(nc.sbuf_tensor("minus_half", [P, 1], F32))
        ident = whole.enter_context(nc.sbuf_tensor("ident", [P, P], F32))
        gates = whole.enter_context(nc.sbuf_tensor("gates", [P, 2], F32))
        tgates = whole.enter_context(nc.sbuf_tensor("tgates", [P, 2], F32))
        attention(nc, x, ctx_in, mask, g_xattn, g_ffn, Wq, Wk, Wv, Wo, cos_sin, acc, xT_hi, xT_lo, xn,
                  stats, moments, rstd, minus_half, ident, gates, tgates)
        feed_forward(nc, gate_q, gate_s, gate_z, up_q, up_s, up_z, down_q, down_s, down_z, nibble,
                     acc, xT_hi, xT_lo, xn, stats, moments, rstd, minus_half, ident, tgates, out)


def attention(nc, x, ctx_in, mask, g_xattn, g_ffn, Wq, Wk, Wv, Wo, cos_sin, acc, xT_hi, xT_lo, xn,
              stats, moments, rstd, minus_half, ident, gates, tgates):
    with ExitStack() as here:
        def sb(name, shape, dt):
            return here.enter_context(nc.sbuf_tensor(name, shape, dt))

        def ps(name, shape):
            return here.enter_context(nc.psum_tensor(name, shape, F32))

        def sem(name):
            return here.enter_context(nc.semaphore(name))

        cT_hi = sb("cT_hi", [P, B, KT, T], F32R)
        cT_lo = sb("cT_lo", [P, B, KT, T], F32R)
        wq_raw = sb("wq_raw", [P, KT, GC], F32)
        wkv_raw = sb("wkv_raw", [P, KT, 2 * D], F32)
        wo_raw = sb("wo_raw", [P, HG, C], F32)
        wq_hi = sb("wq_hi", [P, 2, KT, GC], F32R)
        wq_lo = sb("wq_lo", [P, 2, KT, GC], F32R)
        wkv_hi = sb("wkv_hi", [P, 2, KT, 2 * D], F32R)
        wkv_lo = sb("wkv_lo", [P, 2, KT, 2 * D], F32R)
        wo_hi = sb("wo_hi", [P, 2, HG, C], F32R)
        wo_lo = sb("wo_lo", [P, 2, HG, C], F32R)
        cs_tab = sb("cs_tab", [P, 2, D], F32)
        mask_bytes = sb("mask_bytes", [P, T // 4], U32)
        mask_f = sb("mask_f", [P, T], F32)
        keep = sb("keep", [P, T], F32)
        keepT = sb("keepT", [P, T], F32)
        seen = sb("seen", [P, 1], F32)
        live = sb("live", [P, 1], F32)
        dead = sb("dead", [P, 1], F32)
        q_tab = sb("q_tab", [P, 2, D], F32)
        q_cos = sb("q_cos", [P, HG, D], F32)
        q_sin = sb("q_sin", [P, HG, D], F32)
        k_cos = sb("k_cos", [P, D], F32)
        k_sin = sb("k_sin", [P, D], F32)
        roped = sb("roped", [P, HG + 1, D], F32)
        qT_hi = sb("qT_hi", [P, GC], F32R)
        qT_lo = sb("qT_lo", [P, GC], F32R)
        kT_hi = sb("kT_hi", [P, T], F32R)
        kT_lo = sb("kT_lo", [P, T], F32R)
        v_hi = sb("v_hi", [P, 4, D + 2], F32R)
        v_lo = sb("v_lo", [P, 4, D], F32R)
        capped = sb("capped", [P, GC], F32)
        probs = sb("probs", [P, 2, GC], F32)
        p_hi = sb("p_hi", [P, GC], F32R)
        p_lo = sb("p_lo", [P, GC], F32R)
        rsum = sb("rsum", [P, 2, 2, 1], F32)
        attn = sb("attn", [P, HG * D], F32)
        aT_hi = sb("aT_hi", [P, GC], F32R)
        aT_lo = sb("aT_lo", [P, GC], F32R)
        ctx_raw = [probs[:, 0, :], probs[:, 1, :], capped[:], attn[:]]

        ps_q = ps("ps_q", [P, HG, D])
        ps_kv = ps("ps_kv", [P, 4, D])
        ps_qT = ps("ps_qT", [P, GC])
        ps_s = ps("ps_s", [P, GC])
        ps_pv = ps("ps_pv", [P, 2, 512])
        ps_aT = ps("ps_aT", [P, GC])
        ps_o = ps("ps_o", [P, C])
        pv4 = ps_pv[:, :, 0:2 * (D + 2)].rearrange("p a (h n) -> p a h n", h=2)
        prep_banks = [ps_qT, ps_s, ps_aT, ps_o]

        ld_x = [sem(f"ld_x{b}") for b in range(B)]
        ld_ctx = [sem(f"ld_ctx{i}") for i in range(4)]
        ld_tab, ld_mask, ld_gates = sem("ld_tab"), sem("ld_mask"), sem("ld_gates")
        ld_wq, ld_wkv, ld_wo = sem("ld_wq"), sem("ld_wkv"), sem("ld_wo")
        id_zero, id_done, ones_done, half_done = sem("id_zero"), sem("id_done"), sem("ones_done"), sem("half_done")
        stats_done, moments_done, var_done = sem("stats_done"), sem("moments_done"), sem("var_done")
        rstd_done, xn_done = sem("rstd_done"), sem("xn_done")
        prep_T, prep_hi, prep_lo = sem("prep_T"), sem("prep_hi"), sem("prep_lo")
        mask_step, keep_T, tab_done, tg_done = sem("mask_step"), sem("keep_T"), sem("tab_done"), sem("tg_done")
        wq_rounded, wq_split = sem("wq_rounded"), sem("wq_split")
        wo_rounded, wo_split = sem("wo_rounded"), sem("wo_split")
        q_done, kv_done, tr_done = sem("q_done"), sem("kv_done"), sem("tr_done")
        q_mul, k_mul, q_roped, k_roped = sem("q_mul"), sem("k_mul"), sem("q_roped"), sem("k_roped")
        qk_rounded, qk_split, v_rounded, v_split = sem("qk_rounded"), sem("qk_split"), sem("v_rounded"), sem("v_split")
        s_done, tanh_done, exp_done, masked = sem("s_done"), sem("tanh_done"), sem("exp_done"), sem("masked")
        p_rounded, p_split, pv_done = sem("p_rounded"), sem("p_split"), sem("pv_done")
        rsum_done, norm_done, at_done = sem("rsum_done"), sem("norm_done"), sem("at_done")
        a_rounded, a_split, o_done, acc_done = sem("a_rounded"), sem("a_split"), sem("o_done"), sem("acc_done")

        def all_slots(eng, slot):
            for s in range(B):
                slot(0, 0, s)
            with eng.Fori(0, (SLOTS - 2 * B) // LOOPED) as i:
                for s in range(B, B + LOOPED):
                    slot(i * LOOPED, i * (LOOPED // B), s)
            for s in range(SLOTS - B, SLOTS + 3):
                slot(0, 0, s)

        def runs(s):
            return 0 <= s < SLOTS

        wq_v = Wq.rearrange("(k p) n -> p k n", p=P)
        wk_v = Wk.rearrange("(k p) n -> p k n", p=P)
        wv_v = Wv.rearrange("(k p) n -> p k n", p=P)
        wo_v = Wo.rearrange("(h p) n -> p h n", p=P)

        with nc.Block() as block:

            @block.sync
            def _(sp):
                def load_w(g):
                    wait(sp, wq_split, g * KT)
                    sp.dma_start(wq_raw[:], wq_v[:, :, bass.ds(g * GC, GC)]).then_inc(ld_wq, 16)
                    sp.dma_start(wkv_raw[:, :, 0:D], wk_v[:, :, bass.ds(g * D, D)]).then_inc(ld_wkv, 16)
                    sp.dma_start(wkv_raw[:, :, D:2 * D], wv_v[:, :, bass.ds(g * D, D)]).then_inc(ld_wkv, 16)
                    wait(sp, wo_split, g * HG)
                    sp.dma_start(wo_raw[:], wo_v[:, bass.ds(g * HG, HG), :]).then_inc(ld_wo, 16)

                sp.dma_start(acc[:, 0, :], x[0]).then_inc(ld_x[0], 16)
                sp.dma_start(ctx_raw[0], ctx_in[0]).then_inc(ld_ctx[0], 16)
                sp.dma_start(mask_bytes[:], mask).then_inc(ld_mask, 16)
                sp.dma_start(cs_tab[:], cos_sin).then_inc(ld_tab, 16)
                sp.dma_start(gates[:, 0:1], g_xattn.unsqueeze(0).to_broadcast([P, 1])).then_inc(ld_gates, 16)
                sp.dma_start(gates[:, 1:2], g_ffn.unsqueeze(0).to_broadcast([P, 1])).then_inc(ld_gates, 16)
                load_w(0)
                for b in range(1, B):
                    sp.dma_start(acc[:, b, :], x[b]).then_inc(ld_x[b], 16)
                    if b < 4:
                        sp.dma_start(ctx_raw[b], ctx_in[b]).then_inc(ld_ctx[b], 16)
                for b in range(4, B):
                    sp.wait_ge(prep_T, 2 * (b - 3))
                    sp.dma_start(ctx_raw[b % 4], ctx_in[b]).then_inc(ld_ctx[b % 4], 16)
                load_w(1)
                with sp.Fori(2, KV) as g:
                    load_w(g)

            @block.gpsimd
            def _(pool):
                nc.gpsimd.memset(ident[:], 0.0).then_inc(id_zero, 1)
                nc.gpsimd.memset(minus_half[:], -0.5).then_inc(half_done, 1)
                pool.wait_ge(id_zero, 1)
                nc.gpsimd.affine_select(out=ident[:], in_=ident[:], compare_op=ALU.not_equal, fill=1.0,
                                        base=0, pattern=[[-1, P]], channel_multiplier=1).then_inc(id_done, 1)
                nc.gpsimd.memset(v_hi[:, :, D:D + 2].bitcast(F32), 1.0).then_inc(ones_done, 1)
                pool.wait_ge(half_done, 1)
                for b in range(B):
                    pool.wait_ge(var_done, b + 1)
                    nc.gpsimd.tensor_tensor(rstd[:, b, :], rstd[:, b, :], minus_half[:], ALU.pow).then_inc(rstd_done, 1)

                def split_w(g, part, par):
                    if part < KT:
                        wait(pool, wq_rounded, g * KT + part + 1)
                        nc.gpsimd.tensor_tensor(wq_lo[:, par, part, :], wq_raw[:, part, :],
                                                wq_hi[:, par, part, :].bitcast(F32), ALU.subtract)
                        nc.gpsimd.tensor_tensor(wkv_lo[:, par, part, :], wkv_raw[:, part, :],
                                                wkv_hi[:, par, part, :].bitcast(F32),
                                                ALU.subtract).then_inc(wq_split, 1)
                    else:
                        h = part - KT
                        wait(pool, wo_rounded, g * HG + h + 1)
                        nc.gpsimd.tensor_tensor(wo_lo[:, par, h, :], wo_raw[:, h, :],
                                                wo_hi[:, par, h, :].bitcast(F32),
                                                ALU.subtract).then_inc(wo_split, 1)

                for part in range(B):
                    split_w(0, part, 0)
                pool.wait_ge(tab_done, 1)

                def slot(base, group, s):
                    j = base + s
                    if runs(s + B):
                        split_w(group + s // B + 1, s % B, (s // B + 1) % 2)
                    if runs(s - 1):
                        wait(pool, exp_done, j)
                        pr = probs[:, (s - 1) % 2, :].rearrange("p (h t) -> p h t", h=HG)
                        nc.gpsimd.tensor_tensor(pr, pr, keepT[:].unsqueeze(1).to_broadcast([P, HG, T]),
                                                ALU.mult).then_inc(masked, 1)
                all_slots(pool, slot)

            @block.scalar
            def _(act):
                act.wait_ge(ld_gates, 32)
                nc.scalar.activation(tgates[:], gates[:], ACT.Tanh).then_inc(tg_done, 1)

                def round_w(g, part, par):
                    if part < KT:
                        if part == 0:
                            wait(act, ld_wq, (g + 1) * 16)
                            wait(act, ld_wkv, (g + 1) * 32)
                            wait(act, q_done, (g - 1) * B)
                            wait(act, kv_done, (g - 1) * B)
                        nc.scalar.copy(wq_hi[:, par, part, :], wq_raw[:, part, :])
                        nc.scalar.copy(wkv_hi[:, par, part, :], wkv_raw[:, part, :]).then_inc(wq_rounded, 1)
                    else:
                        h = part - KT
                        if h == 0:
                            wait(act, ld_wo, (g + 1) * 16)
                            wait(act, o_done, (g - 1) * B)
                        nc.scalar.copy(wo_hi[:, par, h, :], wo_raw[:, h, :]).then_inc(wo_rounded, 1)

                for k in range(2 * B):
                    act.wait_ge(prep_T, k + 1)
                    hi = (xT_hi if k % 2 == 0 else cT_hi)[:, k // 2, :, :].rearrange("p k t -> p (k t)")
                    nc.scalar.copy(hi, prep_banks[k % 4][:]).then_inc(prep_hi, 1)
                    if k % 2:
                        round_w(0, k // 2, 0)
                act.wait_ge(ones_done, 1)

                def slot(base, group, s):
                    j = base + s
                    if runs(s - 3):
                        wait(act, at_done, j - 2)
                        wait(act, o_done, j - 3)
                        nc.scalar.copy(aT_hi[:], ps_aT[:]).then_inc(a_rounded, 1)
                    if runs(s + B):
                        round_w(group + s // B + 1, s % B, (s // B + 1) % 2)
                    if runs(s - 1):
                        wait(act, tr_done, j)
                        wait(act, s_done, j - 1)
                        nc.scalar.copy(qT_hi[:], ps_qT[:])
                        nc.scalar.copy(kT_hi[:], ps_kv[:, 2, :]).then_inc(qk_rounded, 1)
                    if runs(s):
                        wait(act, kv_done, j + 1)
                        wait(act, pv_done, j - 3)
                        nc.scalar.copy(v_hi[:, s % 4, 0:D], ps_kv[:, 1, :]).then_inc(v_rounded, 1)
                    if runs(s - 1):
                        wait(act, s_done, j)
                        nc.scalar.activation(capped[:], ps_s[:], ACT.Tanh, scale=ATTN_MULT / MAX_ATTN).then_inc(tanh_done, 1)
                        wait(act, tanh_done, j)
                        wait(act, p_split, j - 2)
                        nc.scalar.activation(probs[:, (s - 1) % 2, :], capped[:], ACT.Exp,
                                             scale=MAX_ATTN).then_inc(exp_done, 1)
                all_slots(act, slot)

            @block.vector
            def _(dve):
                def norm_moments(b):
                    dve.wait_ge(ld_x[b], 16)
                    nc.vector.bn_stats(stats[:, b, :], acc[:, b, :]).then_inc(stats_done, 1)
                    dve.wait_ge(stats_done, b + 1)
                    nc.vector.bn_aggr(moments[:, b, :], stats[:, b, :]).then_inc(moments_done, 1)
                    dve.wait_ge(moments_done, b + 1)
                    nc.vector.tensor_scalar(rstd[:, b, :], moments[:, b, 1:2], EPS, None, ALU.add).then_inc(var_done, 1)

                def norm_apply(b):
                    dve.wait_ge(rstd_done, b + 1)
                    wait(dve, prep_T, 2 * (b - 2) + 1)
                    nc.vector.tensor_scalar(xn[:, b % 2, :], acc[:, b, :], moments[:, b, 0:1], rstd[:, b, :],
                                            ALU.subtract, ALU.mult).then_inc(xn_done, 1)

                def prep_rest(k):
                    dve.wait_ge(prep_hi, k + 1)
                    hi, lo = ((xT_hi, xT_lo) if k % 2 == 0 else (cT_hi, cT_lo))
                    nc.vector.tensor_tensor(lo[:, k // 2, :, :].rearrange("p k t -> p (k t)"), prep_banks[k % 4][:],
                                            hi[:, k // 2, :, :].rearrange("p k t -> p (k t)").bitcast(F32),
                                            ALU.subtract).then_inc(prep_lo, 1)

                for b in range(B + 1):
                    if b < B:
                        norm_moments(b)
                    if b < B:
                        norm_apply(b)
                    if b >= 1:
                        prep_rest(2 * b - 2)
                        prep_rest(2 * b - 1)
                dve.wait_ge(ld_mask, 16)
                nc.vector.tensor_copy(mask_f[:], mask_bytes[:].bitcast(U8)).then_inc(mask_step, 1)
                dve.wait_ge(mask_step, 1)
                nc.vector.reduce_sum(seen[:], mask_f[:], AX_X).then_inc(mask_step, 1)
                dve.wait_ge(mask_step, 2)
                nc.vector.tensor_scalar(live[:], seen[:], 1.0, None, ALU.min).then_inc(mask_step, 1)
                dve.wait_ge(mask_step, 3)
                nc.vector.tensor_scalar(dead[:], live[:], -1.0, 1.0, ALU.mult, ALU.add).then_inc(mask_step, 1)
                dve.wait_ge(mask_step, 4)
                nc.vector.tensor_scalar(keep[:], mask_f[:], dead[:], None, ALU.max).then_inc(mask_step, 1)
                dve.wait_ge(ld_tab, 16)
                nc.vector.tensor_scalar(q_tab[:], cs_tab[:], live[:], None, ALU.mult).then_inc(mask_step, 1)
                dve.wait_ge(keep_T, 1)
                nc.vector.tensor_copy(keepT[:], ps_pv[:, 0, 0:T]).then_inc(tab_done, 1)
                dve.wait_ge(mask_step, 6)
                dve.wait_ge(tg_done, 1)

                def rope(xs, cs, sn, tab, n, mul, done, dst):
                    heads = xs.shape[1]
                    def t(i, lo, hi):
                        return tab[:, i, lo:hi].unsqueeze(1).to_broadcast([P, heads, hi - lo])
                    h = D // 2
                    nc.vector.tensor_tensor(cs, xs, t(0, 0, D), ALU.mult)
                    nc.vector.tensor_tensor(sn[:, :, 0:h], xs[:, :, h:D], t(1, 0, h), ALU.mult)
                    nc.vector.tensor_tensor(sn[:, :, h:D], xs[:, :, 0:h], t(1, h, D), ALU.mult).then_inc(mul, 1)
                    dve.wait_ge(mul, n)
                    nc.vector.tensor_tensor(dst, cs, sn, ALU.add).then_inc(done, 1)

                def slot(base, group, s):
                    j = base + s
                    if runs(s - 3):
                        wait(dve, a_rounded, j - 2)
                        nc.vector.tensor_tensor(aT_lo[:], ps_aT[:], aT_hi[:].bitcast(F32),
                                                ALU.subtract).then_inc(a_split, 1)
                    if runs(s - 1):
                        wait(dve, qk_rounded, j)
                        nc.vector.tensor_tensor(qT_lo[:], ps_qT[:], qT_hi[:].bitcast(F32), ALU.subtract)
                        nc.vector.tensor_tensor(kT_lo[:], ps_kv[:, 2, :], kT_hi[:].bitcast(F32),
                                                ALU.subtract).then_inc(qk_split, 1)
                    if runs(s - 2):
                        par = (s - 2) % 2
                        wait(dve, masked, j - 1)
                        wait(dve, pv_done, j - 2)
                        nc.vector.tensor_copy(p_hi[:], probs[:, par, :]).then_inc(p_rounded, 1)
                        wait(dve, p_rounded, j - 1)
                        nc.vector.tensor_tensor(p_lo[:], probs[:, par, :], p_hi[:].bitcast(F32),
                                                ALU.subtract).then_inc(p_split, 1)
                    if runs(s):
                        wait(dve, q_done, j + 1)
                        wait(dve, tr_done, j)
                        rope(ps_q[:], q_cos[:], q_sin[:], q_tab, j + 1, q_mul, q_roped, roped[:, 0:HG, :])
                        wait(dve, v_rounded, j + 1)
                        nc.vector.tensor_tensor(v_lo[:, s % 4, :], ps_kv[:, 1, :], v_hi[:, s % 4, 0:D].bitcast(F32),
                                                ALU.subtract).then_inc(v_split, 1)
                        rope(ps_kv[:, 0:1, :], k_cos[:].unsqueeze(1), k_sin[:].unsqueeze(1), cs_tab, j + 1,
                             k_mul, k_roped, roped[:, HG:HG + 1, :])
                    if runs(s - 2):
                        wait(dve, pv_done, j - 1)
                        nc.vector.reciprocal(rsum[:], pv4[:, :, :, D:D + 1]).then_inc(rsum_done, 1)
                        wait(dve, rsum_done, j - 1)
                        wait(dve, at_done, j - 2)
                        nc.vector.tensor_tensor(attn[:].rearrange("p (a h d) -> p a h d", a=2, h=2), pv4[:, :, :, 0:D],
                                                rsum[:].to_broadcast([P, 2, 2, D]), ALU.mult).then_inc(norm_done, 1)
                    if runs(s - 3):
                        b = (s - 3) % B
                        wait(dve, o_done, j - 2)
                        wait(dve, acc_done, j - 3)
                        nc.vector.scalar_tensor_tensor(out=acc[:, b, :], in0=ps_o[:], scalar=tgates[:, 0:1],
                                                       in1=acc[:, b, :], op0=ALU.mult,
                                                       op1=ALU.add).then_inc(acc_done, 1)
                all_slots(dve, slot)

            @block.tensor
            def _(pe):
                pe.wait_ge(id_done, 1)
                for k in range(2 * B):
                    b = k // 2
                    if k % 2 == 0:
                        pe.wait_ge(xn_done, b + 1)
                        src = xn[:, b % 2, :]
                    else:
                        pe.wait_ge(ld_ctx[b % 4], 16 * (b // 4 + 1))
                        src = ctx_raw[b % 4]
                    wait(pe, prep_lo, k - 3)
                    for i in range(KT):
                        mm = nc.tensor.transpose(prep_banks[k % 4][:, i * T:(i + 1) * T], src[:, i * P:(i + 1) * P], ident[:])
                    mm.then_inc(prep_T, 1)
                pe.wait_ge(mask_step, 5)
                nc.tensor.transpose(ps_pv[:, 0, 0:T], keep[:], ident[:]).then_inc(keep_T, 1)
                pe.wait_ge(prep_lo, 2 * B)
                pe.wait_ge(tab_done, 1)

                def slot(base, group, s):
                    j = base + s
                    g = group + s // B
                    wpar = (s // B) % 2
                    if runs(s - 1):
                        wait(pe, q_roped, j)
                        wait(pe, k_roped, j)
                        wait(pe, qk_split, j - 1)
                        wait(pe, v_split, j)
                        for h in range(HG):
                            nc.tensor.transpose(ps_qT[:, h * T:(h + 1) * T], roped[:, h, :], ident[:])
                        nc.tensor.transpose(ps_kv[:, 2, :], roped[:, HG, :], ident[:]).then_inc(tr_done, 1)
                    if runs(s):
                        b = s % B
                        if b == 0:
                            wait(pe, wq_split, (g + 1) * KT)
                        for k in range(KT):
                            mm = split_matmul(nc, ps_q[:].rearrange("p h d -> p (h d)"),
                                              xT_hi[:, b, k, :], xT_lo[:, b, k, :],
                                              wq_hi[:, wpar, k, :], wq_lo[:, wpar, k, :], k == 0, k == KT - 1)
                        mm.then_inc(q_done, 1)
                        wait(pe, qk_split, j)
                        for k in range(KT):
                            mm = split_matmul(nc, ps_kv[:, 0:2, :].rearrange("p h d -> p (h d)"),
                                              cT_hi[:, b, k, :], cT_lo[:, b, k, :],
                                              wkv_hi[:, wpar, k, :], wkv_lo[:, wpar, k, :], k == 0, k == KT - 1)
                        mm.then_inc(kv_done, 1)
                    if runs(s - 1):
                        wait(pe, qk_split, j)
                        wait(pe, tanh_done, j - 1)
                        split_matmul(nc, ps_s[:], kT_hi[:], kT_lo[:],
                                     qT_hi[:], qT_lo[:], True, True).then_inc(s_done, 1)
                    if runs(s - 2):
                        vb = (s - 2) % 4
                        wait(pe, p_split, j - 1)
                        wait(pe, norm_done, j - 2)
                        for h in range(HG):
                            o = pv4[:, h // 2, h % 2, :]
                            w_hi, w_lo = p_hi[:, h * T:(h + 1) * T], p_lo[:, h * T:(h + 1) * T]
                            nc.tensor.matmul(o, w_hi, v_hi[:, vb, :], start=True, stop=False)
                            nc.tensor.matmul(o, w_lo, v_hi[:, vb, :], start=False, stop=False)
                            mm = nc.tensor.matmul(o[:, 0:D], w_hi, v_lo[:, vb, :], start=False, stop=True)
                        mm.then_inc(pv_done, 1)
                    if runs(s - 3):
                        wp = ((s - 3) // B) % 2
                        if (s - 3) % B == 0:
                            wait(pe, wo_split, (group + (s - 3) // B + 1) * HG)
                        wait(pe, a_split, j - 2)
                        wait(pe, acc_done, j - 3)
                        for h in range(HG):
                            mm = split_matmul(nc, ps_o[:], aT_hi[:, h * T:(h + 1) * T],
                                              aT_lo[:, h * T:(h + 1) * T],
                                              wo_hi[:, wp, h, :], wo_lo[:, wp, h, :], h == 0, h == HG - 1)
                        mm.then_inc(o_done, 1)
                    if runs(s - 2):
                        wait(pe, norm_done, j - 1)
                        wait(pe, a_split, j - 2)
                        for h in range(HG):
                            mm = nc.tensor.transpose(ps_aT[:, h * T:(h + 1) * T], attn[:, h * D:(h + 1) * D], ident[:])
                        mm.then_inc(at_done, 1)
                all_slots(pe, slot)


def feed_forward(nc, gate_q, gate_s, gate_z, up_q, up_s, up_z, down_q, down_s, down_z, nibble,
                 acc, xT_hi, xT_lo, xn, stats, moments, rstd, minus_half, ident, tgates, out):
    with ExitStack() as here:
        def sb(name, shape, dt):
            return here.enter_context(nc.sbuf_tensor(name, shape, dt))

        def ps(name, shape):
            return here.enter_context(nc.psum_tensor(name, shape, F32))

        def sem(name):
            return here.enter_context(nc.semaphore(name))

        packed = sb("packed", [P, 2, 3, C], U32)
        zeros = sb("zeros", [P, 2, 3 * WORDS], U32)
        scales = sb("scales", [P, 2, 3, C], F16)
        zero_x = sb("zero_x", [P, 3 * C], U32)
        w_full = sb("w_full", [P, 3, C], F32)
        nib = sb("nib", [P, 1 + PACK], U32)
        gu_hi = sb("gu_hi", [P, 2, 2, KT, P], F32R)
        gu_lo = sb("gu_lo", [P, 2, 2, KT, P], F32R)
        wd_hi = sb("wd_hi", [P, NT * C], F32R)
        wd_lo = sb("wd_lo", [P, NT * C], F32R)
        silu = sb("silu", [P, 2, C], F32)
        inner = sb("inner", [P, 2, C], F32)
        h_hi = sb("h_hi", [P, 2, C], F32R)
        h_lo = sb("h_lo", [P, 2, C], F32R)
        k_hi = sb("k_hi", [P, NT * C], F32R)
        k_lo = sb("k_lo", [P, NT * C], F32R)
        y16 = sb("y16", [P, 2, C], F16)

        ps_g = [ps(f"ps_g{i}", [P, C]) for i in range(2)]
        ps_u = [ps(f"ps_u{i}", [P, C]) for i in range(2)]
        ps_d = [ps(f"ps_d{i}", [P, C]) for i in range(4)]

        ld_nib, ld_w = sem("ld_nib"), [sem("ld_w0"), sem("ld_w1")]
        stats2, moments2, var2, rstd2, xn2 = sem("stats2"), sem("moments2"), sem("var2"), sem("rstd2"), sem("xn2")
        prep2_T, prep2_hi, prep2_lo = sem("prep2_T"), sem("prep2_hi"), sem("prep2_lo")
        unpacked, zero_shifted, zero_ready, centred = sem("unpacked"), sem("zero_shifted"), sem("zero_ready"), sem("centred")
        scaled, w_rounded, w_split = sem("scaled"), sem("w_rounded"), sem("w_split")
        gate_done, up_done, silu_done, inner_done = sem("gate_done"), sem("up_done"), sem("silu_done"), sem("inner_done")
        inner_rounded, inner_split = sem("inner_rounded"), sem("inner_split")
        first_down, down_done, y_done, sum_done, stored = (sem("first_down"), sem("down_done"), sem("y_done"),
                                                           sem("sum_done"), sem("stored"))
        LOADS = 2 * KT + 7

        def steps(eng, step):
            step(0, 0)
            step(0, 1)
            with eng.Fori(1, 4) as i:
                for n in range(2):
                    step(i, n)
            for n in range(8, NT + 1):
                step(0, n)

        with nc.Block() as block:

            @block.sync
            def _(sp):
                sp.dma_start(nib[:], nibble).then_inc(ld_nib, 16)

                def load(pair, n):
                    m = pair * 2 + n
                    par = n % 2
                    short = isinstance(pair, int) and n == NT - 1
                    cols, rows = (LAST, LAST) if short else (P, P)
                    wait(sp, w_split, m - 1)
                    for i, (q, z, s) in enumerate(((gate_q, gate_z, gate_s), (up_q, up_z, up_s))):
                        for k in range(KT):
                            src = q[k * 16:(k + 1) * 16, bass.ds(m * P, cols)].unsqueeze(1).to_broadcast([16, PACK, cols])
                            sp.dma_start(packed[:, par, i, k * P:k * P + cols], src).then_inc(ld_w[par], 16)
                        src = z[:, bass.ds(m * (P // PACK), cols // PACK)].unsqueeze(0).to_broadcast([P, KT, cols // PACK])
                        sp.dma_start(zeros[:, par, i * WORDS:(i + 1) * WORDS].rearrange("p (k w) -> p k w", k=KT)[:, :, 0:cols // PACK],
                                     src).then_inc(ld_w[par], 16)
                        src = s[:, bass.ds(m * P, cols)].unsqueeze(0).to_broadcast([P, KT, cols])
                        sp.dma_start(scales[:, par, i, :].rearrange("p (k c) -> p k c", k=KT)[:, :, 0:cols],
                                     src).then_inc(ld_w[par], 16)
                    src = down_q[bass.ds(m * 16, rows // PACK), :].unsqueeze(1).to_broadcast([rows // PACK, PACK, C])
                    sp.dma_start(packed[0:rows, par, 2, :], src).then_inc(ld_w[par], 16)
                    sp.dma_start(zeros[:, par, 2 * WORDS:3 * WORDS],
                                 down_z[bass.ds(m, 1), :].to_broadcast([P, WORDS])).then_inc(ld_w[par], 16)
                    sp.dma_start(scales[:, par, 2, :],
                                 down_s[bass.ds(m, 1), :].to_broadcast([P, C])).then_inc(ld_w[par], 16)

                load(0, 0)
                load(0, 1)
                with sp.Fori(1, 5) as i:
                    for n in range(2):
                        load(i, n)
                load(0, NT - 1)
                for b in range(B):
                    sp.wait_ge(sum_done, b + 1)
                    sp.dma_start(out[b], acc[:, b, :]).then_inc(stored, 16)
                sp.wait_ge(stored, 16 * B)

            @block.gpsimd
            def _(pool):
                for b in range(B):
                    pool.wait_ge(var2, b + 1)
                    nc.gpsimd.tensor_tensor(rstd[:, b, :], rstd[:, b, :], minus_half[:], ALU.pow).then_inc(rstd2, 1)

                def scale(pair, n):
                    m, par = pair * 2 + n, n % 2
                    wait(pool, centred, m + 1)
                    nc.gpsimd.tensor_tensor(w_full[:], w_full[:], scales[:, par, :, :], ALU.mult).then_inc(scaled, 1)
                    wait(pool, w_rounded, m + 1)
                    nc.gpsimd.tensor_tensor(gu_lo[:, par].rearrange("p i k c -> p i (k c)"), w_full[:, 0:2, :],
                                            gu_hi[:, par].rearrange("p i k c -> p i (k c)").bitcast(F32), ALU.subtract)
                    nc.gpsimd.tensor_tensor(wd_lo[:, bass.ds(m * C, C)], w_full[:, 2, :],
                                            wd_hi[:, bass.ds(m * C, C)].bitcast(F32), ALU.subtract).then_inc(w_split, 1)
                with pool.Fori(0, 5) as i:
                    for n in range(2):
                        scale(i, n)
                scale(0, NT - 1)

            @block.scalar
            def _(act):
                def round_w(pair, n):
                    m, par = pair * 2 + n, n % 2
                    wait(act, scaled, m + 1)
                    wait(act, up_done, 2 * (m - 1))
                    nc.scalar.copy(gu_hi[:, par].rearrange("p i k c -> p i (k c)"), w_full[:, 0:2, :])
                    nc.scalar.copy(wd_hi[:, bass.ds(m * C, C)], w_full[:, 2, :]).then_inc(w_rounded, 1)

                round_w(0, 0)
                for b in range(B):
                    act.wait_ge(prep2_T, b + 1)
                    nc.scalar.copy(xT_hi[:, b, :, :].rearrange("p k t -> p (k t)"), ps_d[b % 4][:]).then_inc(prep2_hi, 1)

                def step(pair, n):
                    m = pair * 2 + n
                    rows = LAST if isinstance(pair, int) and n == NT - 1 else P
                    if not isinstance(pair, int) or n + 1 < NT:
                        round_w(pair, n + 1)
                    if not isinstance(pair, int) or n < NT:
                        for half in range(2):
                            wait(act, gate_done, 2 * m + half + 1)
                            nc.scalar.activation(silu[0:rows, half, :], ps_g[half][0:rows, :], ACT.Silu).then_inc(silu_done, 1)
                        for half in range(2):
                            wait(act, inner_done, 2 * m + half + 1)
                            if half == 0:
                                wait(act, first_down, m - 1)
                                dst = h_hi[0:rows, n % 2, :]
                            else:
                                dst = k_hi[0:rows, bass.ds(m * C, C)]
                            nc.scalar.copy(dst, inner[0:rows, half, :]).then_inc(inner_rounded, 1)
                steps(act, step)
                for b in range(B):
                    act.wait_ge(down_done, b + 1)
                    wait(act, sum_done, b - 1)
                    nc.scalar.copy(y16[:, b % 2, :], ps_d[b % 4][:]).then_inc(y_done, 1)

            @block.vector
            def _(dve):
                dve.wait_ge(ld_nib, 16)

                def unpack(pair, n):
                    m, par = pair * 2 + n, n % 2
                    wait(dve, ld_w[par], (pair + n // 2 + 1) * (LOADS * 16))
                    q = packed[:, par].rearrange("p i c -> p (i c)")
                    nc.vector.tensor_scalar(q, q, nib[:, 0:1], 15, ALU.logical_shift_right,
                                            ALU.bitwise_and).then_inc(unpacked, 1)
                    zx = zero_x[:].rearrange("p (w e) -> p w e", e=PACK)
                    nc.vector.tensor_tensor(zx, zeros[:, par, :].unsqueeze(2).to_broadcast([P, 3 * WORDS, PACK]),
                                            nib[:, 1:1 + PACK].unsqueeze(1).to_broadcast([P, 3 * WORDS, PACK]),
                                            ALU.logical_shift_right).then_inc(zero_shifted, 1)
                    wait(dve, zero_shifted, m + 1)
                    nc.vector.tensor_scalar(zero_x[:], zero_x[:], 15, None, ALU.bitwise_and).then_inc(zero_ready, 1)
                    wait(dve, zero_ready, m + 1)
                    wait(dve, w_split, m)
                    nc.vector.scalar_tensor_tensor(out=w_full[:].rearrange("p i c -> p (i c)"), in0=q, scalar=1.0,
                                                   in1=zero_x[:], op0=ALU.subtract,
                                                   op1=ALU.subtract).then_inc(centred, 1)

                def moments_of(b):
                    nc.vector.bn_stats(stats[:, b, :], acc[:, b, :]).then_inc(stats2, 1)
                    dve.wait_ge(stats2, b + 1)
                    nc.vector.bn_aggr(moments[:, b, :], stats[:, b, :]).then_inc(moments2, 1)
                    dve.wait_ge(moments2, b + 1)
                    nc.vector.tensor_scalar(rstd[:, b, :], moments[:, b, 1:2], EPS, None, ALU.add).then_inc(var2, 1)

                unpack(0, 0)
                for b in range(B):
                    moments_of(b)
                for b in range(B + 1):
                    if b < B:
                        dve.wait_ge(rstd2, b + 1)
                        wait(dve, prep2_T, b - 1)
                        nc.vector.tensor_scalar(xn[:, b % 2, :], acc[:, b, :], moments[:, b, 0:1], rstd[:, b, :],
                                                ALU.subtract, ALU.mult).then_inc(xn2, 1)
                    if b >= 1:
                        dve.wait_ge(prep2_hi, b)
                        nc.vector.tensor_tensor(xT_lo[:, b - 1, :, :].rearrange("p k t -> p (k t)"), ps_d[(b - 1) % 4][:],
                                                xT_hi[:, b - 1, :, :].rearrange("p k t -> p (k t)").bitcast(F32),
                                                ALU.subtract).then_inc(prep2_lo, 1)

                def step(pair, n):
                    m = pair * 2 + n
                    rows = LAST if isinstance(pair, int) and n == NT - 1 else P
                    if not isinstance(pair, int) or n + 1 < NT:
                        unpack(pair, n + 1)
                    if not isinstance(pair, int) or n < NT:
                        for half in range(2):
                            wait(dve, silu_done, 2 * m + half + 1)
                            wait(dve, up_done, 2 * m + half + 1)
                            wait(dve, inner_split, 2 * m + half - 1)
                            nc.vector.tensor_tensor(inner[0:rows, half, :], ps_u[half][0:rows, :], silu[0:rows, half, :],
                                                    ALU.mult).then_inc(inner_done, 1)
                        for half in range(2):
                            wait(dve, inner_rounded, 2 * m + half + 1)
                            if half == 0:
                                lo, hi = h_lo[0:rows, n % 2, :], h_hi[0:rows, n % 2, :]
                            else:
                                lo, hi = k_lo[0:rows, bass.ds(m * C, C)], k_hi[0:rows, bass.ds(m * C, C)]
                            nc.vector.tensor_tensor(lo, inner[0:rows, half, :], hi.bitcast(F32),
                                                    ALU.subtract).then_inc(inner_split, 1)
                steps(dve, step)
                for b in range(B):
                    dve.wait_ge(y_done, b + 1)
                    nc.vector.scalar_tensor_tensor(out=acc[:, b, :], in0=y16[:, b % 2, :], scalar=tgates[:, 1:2],
                                                   in1=acc[:, b, :], op0=ALU.mult, op1=ALU.add).then_inc(sum_done, 1)

            @block.tensor
            def _(pe):
                for b in range(B):
                    pe.wait_ge(xn2, b + 1)
                    wait(pe, prep2_lo, b - 3)
                    for i in range(KT):
                        mm = nc.tensor.transpose(ps_d[b % 4][:, i * T:(i + 1) * T], xn[:, b % 2, i * P:(i + 1) * P], ident[:])
                    mm.then_inc(prep2_T, 1)
                pe.wait_ge(prep2_lo, B)

                def step(pair, n):
                    m, par = pair * 2 + n, n % 2
                    cols = LAST if isinstance(pair, int) and n == NT - 1 else P
                    if not isinstance(pair, int) or n < NT:
                        wait(pe, w_split, m + 1)
                        for half in range(2):
                            seqs = slice(half * HALF, (half + 1) * HALF)
                            for i, (bank, free, done) in enumerate(((ps_g[half], silu_done, gate_done),
                                                                    (ps_u[half], inner_done, up_done))):
                                wait(pe, free, 2 * m + half - 1)
                                for k in range(KT):
                                    mm = split_matmul(nc, bank[0:cols, :].rearrange("p (b t) -> p b t", b=HALF),
                                                      gu_hi[:, par, i, k, 0:cols], gu_lo[:, par, i, k, 0:cols],
                                                      xT_hi[:, seqs, k, :], xT_lo[:, seqs, k, :], k == 0, k == KT - 1)
                                mm.then_inc(done, 1)

                def down_first(pair, n, start):
                    m, par = pair * 2 + n, n % 2
                    rows = LAST if isinstance(pair, int) and n == NT - 1 else P
                    last = isinstance(pair, int) and n == NT - 1
                    wait(pe, inner_split, 2 * m + 1)
                    for b in range(HALF):
                        mm = split_matmul(nc, ps_d[b][:], h_hi[0:rows, par, b * T:(b + 1) * T],
                                          h_lo[0:rows, par, b * T:(b + 1) * T],
                                          wd_hi[0:rows, bass.ds(m * C, C)], wd_lo[0:rows, bass.ds(m * C, C)], start, last)
                        if last:
                            mm.then_inc(down_done, 1)
                    return mm

                step(0, 0)
                step(0, 1)
                down_first(0, 0, True).then_inc(first_down, 1)
                with pe.Fori(0, 4) as i:
                    for n in range(2):
                        step(i, n + 2)
                        down_first(i, n + 1, False).then_inc(first_down, 1)
                step(0, NT - 1)
                down_first(0, NT - 2, False).then_inc(first_down, 1)
                down_first(0, NT - 1, False)
                for b in range(HALF, B):
                    pe.wait_ge(inner_split, 2 * NT)
                    pe.wait_ge(y_done, b - HALF + 1)
                    for n in range(NT):
                        rows = LAST if n == NT - 1 else P
                        at = n * C + (b - HALF) * T
                        mm = split_matmul(nc, ps_d[b % 4][:], k_hi[0:rows, at:at + T], k_lo[0:rows, at:at + T],
                                          wd_hi[0:rows, n * C:(n + 1) * C], wd_lo[0:rows, n * C:(n + 1) * C],
                                          n == 0, n == NT - 1)
                    mm.then_inc(down_done, 1)


_OUT = ((B, T, C), "float32")


def rope_tables():
    exponents = np.arange(0, D, 2, dtype=np.float32)
    inv_freq = (np.float32(1.0) / np.float32(10000.0) ** (exponents / np.float32(D))).astype(np.float32)
    phase = np.arange(T, dtype=np.float32)[:, None] * inv_freq[None, :]
    phase = np.concatenate([phase, phase], axis=1).astype(np.float32)
    sign = np.where(np.arange(D) < D // 2, -1.0, 1.0).astype(np.float32)
    return np.stack([np.cos(phase), np.sin(phase) * sign], axis=1).astype(np.float32)


def nibble_table():
    rows = np.arange(P)[:, None] % PACK * 4
    return np.concatenate([rows, np.tile(np.arange(PACK) * 4, (P, 1))], axis=1).astype(np.uint32)


def kernel(x, ctx_4096, mask_1x1xSxS2_bk0, g_xattn, g_ffn, L0_xattn_Wq, L0_xattn_Wk, L0_xattn_Wv, L0_xattn_Wo,
           L0_ffn_gate_qweight, L0_ffn_gate_scales, L0_ffn_gate_zeros, L0_ffn_up_qweight, L0_ffn_up_scales,
           L0_ffn_up_zeros, L0_ffn_down_qweight, L0_ffn_down_scales, L0_ffn_down_zeros):
    import concourse.bacc as bacc
    from concourse.bass_utils import run_bass_kernel_spmd

    def bits(a):
        return np.ascontiguousarray(a).view(np.uint32)

    ins = [("x", np.ascontiguousarray(x)), ("ctx", np.ascontiguousarray(ctx_4096)),
           ("mask", np.ascontiguousarray(mask_1x1xSxS2_bk0).reshape(T, T).view(np.uint32)),
           ("g_xattn", np.ascontiguousarray(g_xattn)), ("g_ffn", np.ascontiguousarray(g_ffn)),
           ("Wq", np.ascontiguousarray(L0_xattn_Wq)), ("Wk", np.ascontiguousarray(L0_xattn_Wk)),
           ("Wv", np.ascontiguousarray(L0_xattn_Wv)), ("Wo", np.ascontiguousarray(L0_xattn_Wo)),
           ("gate_q", bits(L0_ffn_gate_qweight)), ("gate_s", np.ascontiguousarray(L0_ffn_gate_scales)),
           ("gate_z", bits(L0_ffn_gate_zeros)),
           ("up_q", bits(L0_ffn_up_qweight)), ("up_s", np.ascontiguousarray(L0_ffn_up_scales)),
           ("up_z", bits(L0_ffn_up_zeros)),
           ("down_q", bits(L0_ffn_down_qweight)), ("down_s", np.ascontiguousarray(L0_ffn_down_scales)),
           ("down_z", bits(L0_ffn_down_zeros)),
           ("cos_sin", rope_tables()), ("nibble", nibble_table())]
    nc = bacc.Bacc("TRN2", target_bir_lowering=False, num_devices=1, dynamic_dma_scratch_size=256)
    arrays, args = {}, []
    for name, a in ins:
        arrays[f"in_{name}"] = a
        args.append(nc.dram_tensor(f"in_{name}", a.shape, mybir.dt.from_np(a.dtype), kind="ExternalInput").ap())
    args.append(nc.dram_tensor("out_dram", _OUT[0], F32, kind="ExternalOutput").ap())
    flamingo_block(nc, *args)
    r = run_bass_kernel_spmd(nc, [arrays], core_ids=[0])
    return r.results[0]["out_dram"]
```

```python
from contextlib import ExitStack

import numpy as np

import concourse.bass as bass
from concourse import mybir

ALU = mybir.AluOpType
ACT = mybir.ActivationFunctionType
F32 = mybir.dt.float32
F32R = mybir.dt.float32r
F16 = mybir.dt.float16
U32 = mybir.dt.uint32
U8 = mybir.dt.uint8
AX_X = mybir.AxisListType.X

P = 128
B = 8
T = 128
C = 512
KT = C // P
KV = 8
HG = 4
D = 128
GC = HG * D
SLOTS = KV * B
LOOPED = 16
INTER = 1376
NT = 11
LAST = INTER - (NT - 1) * P
PACK = 8
WORDS = C // PACK
HALF = B // 2
ATTN_MULT = 0.08838834764831845
MAX_ATTN = 30.0
EPS = 1e-5
DVE_ADDS = 3
BYTES = {F32: 4, F32R: 4, U32: 4, F16: 2}
SBUF_BASE = 384
TAIL = SLOTS - B


def wait(eng, s, n):
    if not isinstance(n, int) or n > 0:
        eng.wait_ge(s, n)


def split_matmul(nc, out, w_hi, w_lo, m_hi, m_lo, first, last):
    nc.tensor.matmul(out, w_hi, m_hi, start=first, stop=False)
    nc.tensor.matmul(out, w_hi, m_lo, start=False, stop=False)
    return nc.tensor.matmul(out, w_lo, m_hi, start=False, stop=last)


def flamingo_block(nc, x, ctx_in, mask, g_xattn, g_ffn, Wq, Wk, Wv, Wo,
                   gate_q, gate_s, gate_z, up_q, up_s, up_z, down_q, down_s, down_z,
                   cos_sin, nibble, out):
    with ExitStack() as here:
        at = [SBUF_BASE]

        def over(name, shape, dt, offset):
            return nc.alloc_sbuf_tensor_at(name, shape, dt, offset=offset)

        def sb(name, shape, dt):
            offset = at[0]
            at[0] += (int(np.prod(shape[1:])) * BYTES[dt] + 31) // 32 * 32
            return over(name, shape, dt, offset)

        def ps(name, shape):
            return here.enter_context(nc.psum_tensor(name, shape, F32))

        def sem(name):
            return here.enter_context(nc.semaphore(name))

        acc = sb("acc", [P, B, C], F32)
        xT_hi = sb("xT_hi", [P, B, KT, T], F32R)
        xT_lo = sb("xT_lo", [P, B, KT, T], F32R)
        xn = sb("xn", [P, 2, C], F32)
        stats = sb("stats", [P, B, 6], F32)
        moments = sb("moments", [P, B, 2], F32)
        rstd = sb("rstd", [P, B, 1], F32)
        minus_half = sb("minus_half", [P, 1], F32)
        ident = sb("ident", [P, P], F32)
        gates = sb("gates", [P, 2], F32)
        tgates = sb("tgates", [P, 2], F32)
        nib = sb("nib", [P, 1 + PACK], U32)

        raw_at = at[0]
        wq_raw = sb("wq_raw", [P, KT, GC], F32)
        wkv_raw = sb("wkv_raw", [P, KT, 2 * D], F32)
        wo_raw_at = at[0]
        wo_raw = sb("wo_raw", [P, HG, C], F32)
        wq_hi, wq_lo, wkv_hi, wkv_lo, wo_hi, wo_lo = [], [], [], [], [], []
        qkv_at, wo_at = [], []

        def place_weights(par):
            qkv_at.append(at[0])
            wq_hi.append(sb(f"wq_hi{par}", [P, KT, GC], F32R))
            wq_lo.append(sb(f"wq_lo{par}", [P, KT, GC], F32R))
            wkv_hi.append(sb(f"wkv_hi{par}", [P, KT, 2 * D], F32R))
            wkv_lo.append(sb(f"wkv_lo{par}", [P, KT, 2 * D], F32R))
            wo_at.append(at[0])
            wo_hi.append(sb(f"wo_hi{par}", [P, HG, C], F32R))
            wo_lo.append(sb(f"wo_lo{par}", [P, HG, C], F32R))

        place_weights(0)
        cT_hi_at = at[0]
        cT_hi = sb("cT_hi", [P, B, KT, T], F32R)
        q_cos = sb("q_cos", [P, HG, D], F32)
        q_sin = sb("q_sin", [P, HG, D], F32)
        capped = sb("capped", [P, GC], F32)
        cT_lo_at = at[0]
        cT_lo = sb("cT_lo", [P, B, KT, T], F32R)
        p_hi = sb("p_hi", [P, GC], F32R)
        p_lo = sb("p_lo", [P, GC], F32R)
        attn = sb("attn", [P, GC], F32)
        place_weights(1)
        small_at = at[0]
        probs = sb("probs", [P, 2, GC], F32)
        roped = sb("roped", [P, HG + 1, D], F32)
        qT_hi = sb("qT_hi", [P, GC], F32R)
        qT_lo = sb("qT_lo", [P, GC], F32R)
        kT_hi = sb("kT_hi", [P, T], F32R)
        kT_lo = sb("kT_lo", [P, T], F32R)
        v_hi = sb("v_hi", [P, 4, D], F32R)
        v_lo = sb("v_lo", [P, 4, D], F32R)
        aT_hi = sb("aT_hi", [P, GC], F32R)
        aT_lo = sb("aT_lo", [P, GC], F32R)
        k_cos = sb("k_cos", [P, D], F32)
        k_sin = sb("k_sin", [P, D], F32)
        cs_tab = sb("cs_tab", [P, 2, D], F32)
        q_tab = sb("q_tab", [P, 2, D], F32)
        mask_bytes = sb("mask_bytes", [P, T // 4], U32)
        mask_f = sb("mask_f", [P, T], F32)
        keep = mask_f
        keepT = sb("keepT", [P, T], F32)
        seen = sb("seen", [P, 1], F32)
        live = sb("live", [P, 1], F32)
        dead = sb("dead", [P, 1], F32)
        ones = sb("ones", [P, P], F32R)
        r_tot = sb("r_tot", [P, GC], F32)
        ctx_rows = over("ctx_rows", [P, C], F32, wo_at[1] + (2 * HG - 1) * C * 4)
        ctx_raw = [capped[:], attn[:], ctx_rows[:], xn[:, 1, :]]

        packed = over("packed", [P, 2, 3, C], U32, raw_at)
        zeros = over("zeros", [P, 2, 3 * WORDS], U32, wo_raw_at)
        scales = over("scales", [P, 2, 3, C], F16, wo_raw_at + 6 * WORDS * 4)
        zero_x = over("zero_x", [P, 3 * C], U32, qkv_at[0])
        w_full = over("w_full", [P, 2, 3, C], F32, qkv_at[0] + 3 * C * 4)
        gu_hi = over("gu_hi", [P, 2, 2, KT, P], F32R, wo_at[0])
        gu_lo = over("gu_lo", [P, 2, 2, KT, P], F32R, wo_at[0] + 4 * KT * P * 4)
        wd_hi = over("wd_hi", [P, NT * C], F32R, cT_hi_at)
        wd_lo = over("wd_lo", [P, NT * C], F32R, cT_lo_at)
        silu = over("silu", [P, 2, C], F32, qkv_at[1])
        inner = over("inner", [P, 2, C], F32, qkv_at[1] + 2 * C * 4)
        h_hi = over("h_hi", [P, 2, C], F32R, qkv_at[1] + 4 * C * 4)
        h_lo = over("h_lo", [P, 2, C], F32R, qkv_at[1] + 6 * C * 4)
        y16 = over("y16", [P, 2, C], F16, qkv_at[1] + 8 * C * 4)
        share = over("share", [P, C], F32, qkv_at[0] + 9 * C * 4)
        k_hi = over("k_hi", [P, NT * C], F32R, qkv_at[1] + 9 * C * 4)
        k_lo = over("k_lo", [P, NT * C], F32R, small_at)

        bank_q = ps("bank_q", [P, C])
        bank_kv = ps("bank_kv", [P, C])
        ps_q = bank_q[:].rearrange("p (h d) -> p h d", h=HG)
        ps_kv = bank_kv[:].rearrange("p (h d) -> p h d", h=4)
        ps_qT = ps("ps_qT", [P, GC])
        ps_s = ps("ps_s", [P, GC])
        ps_pv = ps("ps_pv", [P, GC])
        ps_tot = ps("ps_tot", [P, GC])
        ps_x = ps("ps_x", [P, C])
        ps_o = ps("ps_o", [P, C])
        ps_g = [bank_q[:], ps_qT[:]]
        ps_u = [bank_kv[:], ps_s[:]]
        ps_d = [ps_pv[:], ps_tot[:], ps_x[:], ps_o[:]]

        def norm2_bank(b):
            return ps_d[2] if b < B - 2 else ps_d[b - (B - 2)]

        ld_x = [sem(f"ld_x{b}") for b in range(B)]
        ld_ctx = [sem(f"ld_ctx{i}") for i in range(4)]
        ld_tab, ld_mask, ld_gates = sem("ld_tab"), sem("ld_mask"), sem("ld_gates")
        ld_wq, ld_wkv, ld_wo = sem("ld_wq"), sem("ld_wkv"), sem("ld_wo")
        id_zero, id_done, ones_done, half_done = sem("id_zero"), sem("id_done"), sem("ones_done"), sem("half_done")
        stats_done, moments_done, var_done = sem("stats_done"), sem("moments_done"), sem("var_done")
        rstd_done, xn_done = sem("rstd_done"), sem("xn_done")
        x_T, x_hi, x_lo = sem("x_T"), sem("x_hi"), sem("x_lo")
        ctx_T, ctx_hi, ctx_lo = sem("ctx_T"), sem("ctx_hi"), sem("ctx_lo")
        ld_wq0 = [sem("ld_wq0_a"), sem("ld_wq0_b")]
        wq0_rounded, wq0_split, wkv0_rounded, wkv0_split = (sem("wq0_rounded"), sem("wq0_split"),
                                                            sem("wkv0_rounded"), sem("wkv0_split"))
        mask_step, keep_T, tab_done, tg_done = sem("mask_step"), sem("keep_T"), sem("tab_done"), sem("tg_done")
        wq_rounded, wq_split = sem("wq_rounded"), sem("wq_split")
        wo_rounded, wo_split = sem("wo_rounded"), sem("wo_split")
        q_done, kv_done, tr_done = sem("q_done"), sem("kv_done"), sem("tr_done")
        q_mul, k_mul, q_roped, k_roped = sem("q_mul"), sem("k_mul"), sem("q_roped"), sem("k_roped")
        qk_rounded, qk_split, v_rounded, v_split = sem("qk_rounded"), sem("qk_split"), sem("v_rounded"), sem("v_split")
        s_done, tanh_done, exp_done, masked = sem("s_done"), sem("tanh_done"), sem("exp_done"), sem("masked")
        p_rounded, p_split, pv_done = sem("p_rounded"), sem("p_split"), sem("pv_done")
        tot_done, inverted, norm_done = sem("tot_done"), sem("inverted"), sem("norm_done")
        a_rounded, a_split, o_done, acc_done = sem("a_rounded"), sem("a_split"), sem("o_done"), sem("acc_done")

        share_scaled = sem("share_scaled")
        ld_nib, ld_q, ld_zs = sem("ld_nib"), [sem("ld_q0"), sem("ld_q1")], [sem("ld_zs0"), sem("ld_zs1")]
        stats2, moments2, var2, rstd2, xn2 = sem("stats2"), sem("moments2"), sem("var2"), sem("rstd2"), sem("xn2")
        prep2_T, prep2_hi, prep2_lo = sem("prep2_T"), sem("prep2_hi"), sem("prep2_lo")
        unpacked, zero_shifted, zero_ready, centred = sem("unpacked"), sem("zero_shifted"), sem("zero_ready"), sem("centred")
        scaled, w_rounded, w_split = sem("scaled"), sem("w_rounded"), sem("w_split")
        gate_done, up_done, silu_done, inner_done = sem("gate_done"), sem("up_done"), sem("silu_done"), sem("inner_done")
        inner_rounded, inner_split = sem("inner_rounded"), sem("inner_split")
        first_down, down_done, y_done, sum_done, stored = (sem("first_down"), sem("down_done"), sem("y_done"),
                                                           sem("sum_done"), sem("stored"))
        Q_LOADS, ZS_LOADS = 2 * KT + 1, 6

        def steps(eng, step):
            step(0, 0)
            step(0, 1)
            with eng.Fori(1, 4) as i:
                for n in range(2):
                    step(i, n)
            for n in range(8, NT + 1):
                step(0, n)

        early_parts = [[(0, 4), (0, 5)], [(0, 6), (0, 7)], [(1, 0)], [(1, 1)], [(1, 2)], [(1, 3)],
                       [(1, 4), (1, 5)], [(1, 6), (1, 7)]]

        def raw_of(b):
            return b if b < 2 else 2 + b % 2

        def all_slots(eng, slot):
            for s in range(B):
                slot(0, 0, s)
            with eng.Fori(0, (SLOTS - 2 * B) // LOOPED) as i:
                for s in range(B, B + LOOPED):
                    slot(i * LOOPED, i * (LOOPED // B), s)
            for s in range(SLOTS - B, SLOTS + 3):
                slot(0, 0, s)

        def runs(s):
            return 0 <= s < SLOTS

        wq_v = Wq.rearrange("(k p) n -> p k n", p=P)
        wk_v = Wk.rearrange("(k p) n -> p k n", p=P)
        wv_v = Wv.rearrange("(k p) n -> p k n", p=P)
        wo_v = Wo.rearrange("(h p) n -> p h n", p=P)

        with nc.Block() as block:

            @block.sync
            def _(sp):
                def load_wqkv(g):
                    wait(sp, wq_split, (g - 1) * KT)
                    sp.dma_start(wq_raw[:], wq_v[:, :, bass.ds(g * GC, GC)]).then_inc(ld_wq, 16)
                    sp.dma_start(wkv_raw[:, :, 0:D], wk_v[:, :, bass.ds(g * D, D)]).then_inc(ld_wkv, 16)
                    sp.dma_start(wkv_raw[:, :, D:2 * D], wv_v[:, :, bass.ds(g * D, D)]).then_inc(ld_wkv, 16)

                def load_wo(g):
                    wait(sp, wo_split, g * HG)
                    sp.dma_start(wo_raw[:], wo_v[:, bass.ds(g * HG, HG), :]).then_inc(ld_wo, 16)

                def load_ctx(b):
                    i = raw_of(b)
                    wait(sp, ctx_lo, b - 1 if b >= 4 else 0)
                    sp.dma_start(ctx_raw[i], ctx_in[b]).then_inc(ld_ctx[i], 16)

                def load_x(b):
                    sp.dma_start(acc[:, b, :], x[b]).then_inc(ld_x[b], 16)

                load_x(0)
                sp.dma_start(mask_bytes[:], mask).then_inc(ld_mask, 16)
                load_ctx(0)
                for i in range(2):
                    ks = slice(2 * i, 2 * i + 2)
                    sp.dma_start(wq_raw[:, ks, :], wq_v[:, ks, 0:GC]).then_inc(ld_wq0[i], 16)
                sp.dma_start(cs_tab[:], cos_sin).then_inc(ld_tab, 16)
                load_x(1)
                sp.dma_start(wkv_raw[:, :, 0:D], wk_v[:, :, 0:D]).then_inc(ld_wkv, 16)
                sp.dma_start(wkv_raw[:, :, D:2 * D], wv_v[:, :, 0:D]).then_inc(ld_wkv, 16)
                load_ctx(1)
                sp.dma_start(gates[:, 0:1], g_xattn.unsqueeze(0).to_broadcast([P, 1])).then_inc(ld_gates, 16)
                sp.dma_start(gates[:, 1:2], g_ffn.unsqueeze(0).to_broadcast([P, 1])).then_inc(ld_gates, 16)
                load_x(2)
                load_ctx(2)
                sp.dma_start(wo_raw[:], wo_v[:, 0:HG, :]).then_inc(ld_wo, 16)
                for b in range(3, B):
                    load_x(b)
                load_ctx(3)
                sp.wait_ge(wq0_split, KT)
                sp.wait_ge(wkv0_split, 1)
                sp.dma_start(nib[:], nibble).then_inc(ld_nib, 16)
                load_wqkv(1)
                load_ctx(4)
                load_ctx(5)
                load_wo(1)
                load_ctx(6)
                load_ctx(7)
                with sp.Fori(2, KV) as g:
                    load_wqkv(g)
                    load_wo(g)

                def load_q(pair, n):
                    m = pair * 2 + n
                    par = n % 2
                    cols, rows = (LAST, LAST) if isinstance(pair, int) and n == NT - 1 else (P, P)
                    wait(sp, scaled, m - 1)
                    for i, q in enumerate((gate_q, up_q)):
                        for k in range(KT):
                            src = q[k * 16:(k + 1) * 16, bass.ds(m * P, cols)].unsqueeze(1).to_broadcast([16, PACK, cols])
                            sp.dma_start(packed[:, par, i, k * P:k * P + cols], src).then_inc(ld_q[par], 16)
                    src = down_q[bass.ds(m * 16, rows // PACK), :].unsqueeze(1).to_broadcast([rows // PACK, PACK, C])
                    sp.dma_start(packed[0:rows, par, 2, :], src).then_inc(ld_q[par], 16)

                def load_zs(pair, n):
                    m = pair * 2 + n
                    par = n % 2
                    cols = LAST if isinstance(pair, int) and n == NT - 1 else P
                    for i, (z, s) in enumerate(((gate_z, gate_s), (up_z, up_s))):
                        src = z[:, bass.ds(m * (P // PACK), cols // PACK)].unsqueeze(0).to_broadcast([P, KT, cols // PACK])
                        sp.dma_start(zeros[:, par, i * WORDS:(i + 1) * WORDS].rearrange("p (k w) -> p k w", k=KT)[:, :, 0:cols // PACK],
                                     src).then_inc(ld_zs[par], 16)
                        src = s[:, bass.ds(m * P, cols)].unsqueeze(0).to_broadcast([P, KT, cols])
                        sp.dma_start(scales[:, par, i, :].rearrange("p (k c) -> p k c", k=KT)[:, :, 0:cols],
                                     src).then_inc(ld_zs[par], 16)
                    sp.dma_start(zeros[:, par, 2 * WORDS:3 * WORDS],
                                 down_z[bass.ds(m, 1), :].to_broadcast([P, WORDS])).then_inc(ld_zs[par], 16)
                    sp.dma_start(scales[:, par, 2, :],
                                 down_s[bass.ds(m, 1), :].to_broadcast([P, C])).then_inc(ld_zs[par], 16)

                sp.wait_ge(wq_split, (KV - 1) * KT)
                load_q(0, 0)
                load_q(0, 1)
                sp.wait_ge(wo_split, KV * HG)
                load_zs(0, 0)
                load_zs(0, 1)
                with sp.Fori(1, 5) as i:
                    for n in range(2):
                        load_q(i, n)
                        load_zs(i, n)
                load_q(0, NT - 1)
                load_zs(0, NT - 1)
                for b in range(B):
                    sp.wait_ge(sum_done, b + 1)
                    sp.dma_start(out[b], acc[:, b, :]).then_inc(stored, 16)
                sp.wait_ge(stored, 16 * B)

            @block.gpsimd
            def _(pool):
                nc.gpsimd.memset(ident[:], 0.0).then_inc(id_zero, 1)
                nc.gpsimd.memset(minus_half[:], -0.5).then_inc(half_done, 1)
                pool.wait_ge(id_zero, 1)
                nc.gpsimd.affine_select(out=ident[:], in_=ident[:], compare_op=ALU.not_equal, fill=1.0,
                                        base=0, pattern=[[-1, P]], channel_multiplier=1).then_inc(id_done, 1)
                nc.gpsimd.memset(ones[:].bitcast(F32), 1.0).then_inc(ones_done, 1)
                pool.wait_ge(half_done, 1)

                def invert_std(b):
                    pool.wait_ge(var_done, b + 1)
                    nc.gpsimd.tensor_tensor(rstd[:, b, :], rstd[:, b, :], minus_half[:], ALU.pow).then_inc(rstd_done, 1)

                def prep(b):
                    for copied, hi, lo, rounded, done in ((xn[:, 0, :], xT_hi, xT_lo, x_hi, x_lo),
                                                          (ctx_raw[raw_of(b)], cT_hi, cT_lo, ctx_hi, ctx_lo)):
                        pool.wait_ge(rounded, b + 1)
                        nc.gpsimd.tensor_tensor(lo[:, b, :, :].rearrange("p k t -> p (k t)"), copied,
                                                hi[:, b, :, :].rearrange("p k t -> p (k t)").bitcast(F32),
                                                ALU.subtract).then_inc(done, 1)

                def split_w(g, part, par):
                    if part < KT:
                        wait(pool, wq_rounded, (g - 1) * KT + part + 1)
                        nc.gpsimd.tensor_tensor(wq_lo[par][:, part, :], wq_raw[:, part, :],
                                                wq_hi[par][:, part, :].bitcast(F32), ALU.subtract)
                        nc.gpsimd.tensor_tensor(wkv_lo[par][:, part, :], wkv_raw[:, part, :],
                                                wkv_hi[par][:, part, :].bitcast(F32),
                                                ALU.subtract).then_inc(wq_split, 1)
                    else:
                        h = part - KT
                        wait(pool, wo_rounded, g * HG + h + 1)
                        nc.gpsimd.tensor_tensor(wo_lo[par][:, h, :], wo_raw[:, h, :],
                                                wo_hi[par][:, h, :].bitcast(F32),
                                                ALU.subtract).then_inc(wo_split, 1)

                invert_std(0)
                invert_std(1)
                pool.wait_ge(wkv0_rounded, 1)
                nc.gpsimd.tensor_tensor(wkv_lo[0][:, :, :], wkv_raw[:], wkv_hi[0][:, :, :].bitcast(F32),
                                        ALU.subtract).then_inc(wkv0_split, 1)
                invert_std(2)

                def invert_std2(b):
                    pool.wait_ge(var2, b + 1)
                    nc.gpsimd.tensor_tensor(rstd[:, b, :], rstd[:, b, :], minus_half[:], ALU.pow).then_inc(rstd2, 1)

                def scale(pair, n):
                    m, par = pair * 2 + n, n % 2
                    wait(pool, centred, m + 1)
                    nc.gpsimd.tensor_tensor(w_full[:, par], w_full[:, par], scales[:, par, :, :], ALU.mult).then_inc(scaled, 1)

                def rest(pair, n):
                    m, par = pair * 2 + n, n % 2
                    wait(pool, w_rounded, m + 1)
                    nc.gpsimd.tensor_tensor(gu_lo[:, par].rearrange("p i k c -> p i (k c)"), w_full[:, par, 0:2, :],
                                            gu_hi[:, par].rearrange("p i k c -> p i (k c)").bitcast(F32), ALU.subtract)
                    nc.gpsimd.tensor_tensor(wd_lo[:, bass.ds(m * C, C)], w_full[:, par, 2, :],
                                            wd_hi[:, bass.ds(m * C, C)].bitcast(F32), ALU.subtract).then_inc(w_split, 1)
                def p_rest(j):
                    pool.wait_ge(p_rounded, j - 1)
                    nc.gpsimd.tensor_tensor(p_lo[:], probs[:, j % 2, :], p_hi[:].bitcast(F32),
                                            ALU.subtract).then_inc(p_split, 1)

                def slot(base, group, s):
                    j = base + s
                    if TAIL < s < SLOTS + 3:
                        b = (s - 4) % B
                        pool.wait_ge(share_scaled, s - TAIL)
                        nc.gpsimd.tensor_tensor(acc[:, b, :], acc[:, b, :], share[:], ALU.add).then_inc(acc_done, 1)
                    if TAIL <= s < SLOTS:
                        p_rest(s)
                    if runs(s - 3):
                        wait(pool, a_rounded, j - 2)
                        nc.gpsimd.tensor_tensor(aT_lo[:], attn[:], aT_hi[:].bitcast(F32),
                                                ALU.subtract).then_inc(a_split, 1)
                    if s == 0:
                        prep(1)
                    if s + 2 < B:
                        prep(s + 2)
                    if s >= B and runs(s + B):
                        split_w(group + s // B + 1, s % B, (s // B + 1) % 2)
                    if s >= DVE_ADDS and runs(s):
                        wait(pool, q_mul, j + 1)
                        wait(pool, tr_done, j)
                        nc.gpsimd.tensor_tensor(roped[:, 0:HG, :], q_cos[:], q_sin[:], ALU.add).then_inc(q_roped, 1)
                    if s == 1:
                        pool.wait_ge(tab_done, 1)
                    if runs(s - 1):
                        wait(pool, exp_done, j)
                        pr = probs[:, (s - 1) % 2, :].rearrange("p (h t) -> p h t", h=HG)
                        nc.gpsimd.tensor_tensor(pr, pr, keepT[:].unsqueeze(1).to_broadcast([P, HG, T]),
                                                ALU.mult).then_inc(masked, 1)
                    if s + 3 < B:
                        invert_std(s + 3)
                    if s < B:
                        for head, part in early_parts[s]:
                            split_w(head, part, head)
                    if s == TAIL + 9:
                        scale(0, 1)
                    if s >= TAIL + 4:
                        invert_std2(s - TAIL - 4)
                    if s == TAIL + 4:
                        scale(0, 0)
                    if s == TAIL + 6:
                        rest(0, 0)
                    if s == TAIL + 10:
                        invert_std2(7)
                all_slots(pool, slot)
                rest(0, 1)
                with pool.Fori(1, 5) as i:
                    for n in range(2):
                        scale(i, n)
                        rest(i, n)
                scale(0, NT - 1)
                rest(0, NT - 1)

            @block.scalar
            def _(act):
                def round_w(g, part, par):
                    if part < KT:
                        if part == 0:
                            wait(act, ld_wq, g * 16)
                            wait(act, ld_wkv, (g + 1) * 32)
                            wait(act, q_done, (g - 1) * B)
                            wait(act, kv_done, (g - 1) * B)
                        nc.scalar.copy(wq_hi[par][:, part, :], wq_raw[:, part, :])
                        nc.scalar.copy(wkv_hi[par][:, part, :], wkv_raw[:, part, :]).then_inc(wq_rounded, 1)
                    else:
                        h = part - KT
                        if h == 0:
                            wait(act, ld_wo, (g + 1) * 16)
                            wait(act, o_done, (g - 1) * B)
                        nc.scalar.copy(wo_hi[par][:, h, :], wo_raw[:, h, :]).then_inc(wo_rounded, 1)

                def prep(b):
                    act.wait_ge(x_T, b + 1)
                    if b > 0:
                        nc.scalar.copy(xn[:, 0, :], ps_x[:])
                    nc.scalar.copy(xT_hi[:, b, :, :].rearrange("p k t -> p (k t)"), ps_x[:]).then_inc(x_hi, 1)
                    act.wait_ge(ctx_T, b + 1)
                    if b > 0:
                        nc.scalar.copy(ctx_raw[raw_of(b)], ps_o[:])
                    nc.scalar.copy(cT_hi[:, b, :, :].rearrange("p k t -> p (k t)"), ps_o[:]).then_inc(ctx_hi, 1)

                prep(0)
                for k in range(KT):
                    act.wait_ge(ld_wq0[k // 2], 16)
                    nc.scalar.copy(wq_hi[0][:, k, :], wq_raw[:, k, :]).then_inc(wq0_rounded, 1)
                act.wait_ge(ld_wkv, 32)
                nc.scalar.copy(wkv_hi[0][:, :, :], wkv_raw[:]).then_inc(wkv0_rounded, 1)
                act.wait_ge(ld_gates, 32)
                nc.scalar.activation(tgates[:], gates[:], ACT.Tanh).then_inc(tg_done, 1)

                def round_ffn(pair, n):
                    m, par = pair * 2 + n, n % 2
                    wait(act, scaled, m + 1)
                    wait(act, up_done, 2 * (m - 1))
                    nc.scalar.copy(gu_hi[:, par].rearrange("p i k c -> p i (k c)"), w_full[:, par, 0:2, :])
                    nc.scalar.copy(wd_hi[:, bass.ds(m * C, C)], w_full[:, par, 2, :]).then_inc(w_rounded, 1)

                def norm2_hi(b):
                    act.wait_ge(prep2_T, b + 1)
                    nc.scalar.copy(xT_hi[:, b, :, :].rearrange("p k t -> p (k t)"), norm2_bank(b)).then_inc(prep2_hi, 1)

                def slot(base, group, s):
                    j = base + s
                    if TAIL < s < SLOTS + 3:
                        act.wait_ge(o_done, s - 3)
                        act.wait_ge(acc_done, s - 4)
                        act.wait_ge(kv_done, TAIL)
                        nc.scalar.activation(share[:], ps_o[:], ACT.Copy, scale=tgates[:, 0:1]).then_inc(share_scaled, 1)
                    if runs(s - 1):
                        wait(act, tr_done, j)
                        wait(act, s_done, j - 1)
                        nc.scalar.copy(qT_hi[:], ps_qT[:])
                        nc.scalar.copy(kT_hi[:], ps_kv[:, 2, :]).then_inc(qk_rounded, 1)
                    if runs(s - 2):
                        wait(act, masked, j - 1)
                        wait(act, pv_done, j - 2)
                        nc.scalar.copy(p_hi[:], probs[:, (s - 2) % 2, :]).then_inc(p_rounded, 1)
                    if runs(s - 3):
                        wait(act, norm_done, j - 2)
                        wait(act, o_done, j - 3)
                        nc.scalar.copy(aT_hi[:], attn[:]).then_inc(a_rounded, 1)
                    if s >= B and runs(s + B):
                        round_w(group + s // B + 1, s % B, (s // B + 1) % 2)
                    if s == 0:
                        prep(1)
                    elif s + 2 < B:
                        prep(s + 2)
                    elif s >= TAIL + 5:
                        norm2_hi(s - TAIL - 5)
                    if runs(s):
                        wait(act, kv_done, j + 1)
                        wait(act, pv_done, j - 3)
                        nc.scalar.copy(v_hi[:, s % 4, :], ps_kv[:, 1, :]).then_inc(v_rounded, 1)
                    if s == 0:
                        prep(2)
                    if runs(s - 1):
                        wait(act, s_done, j)
                        nc.scalar.activation(capped[:], ps_s[:], ACT.Tanh, scale=ATTN_MULT / MAX_ATTN).then_inc(tanh_done, 1)
                        wait(act, tanh_done, j)
                        wait(act, p_split, j - 2)
                        nc.scalar.activation(probs[:, (s - 1) % 2, :], capped[:], ACT.Exp,
                                             scale=MAX_ATTN).then_inc(exp_done, 1)
                    if s < B:
                        for head, part in early_parts[s]:
                            round_w(head, part, head)
                    if s == TAIL + 5:
                        act.wait_ge(o_done, TAIL)
                        act.wait_ge(kv_done, TAIL + 1)
                        round_ffn(0, 0)
                    if s == TAIL + 10:
                        round_ffn(0, 1)
                        norm2_hi(6)
                all_slots(act, slot)
                norm2_hi(7)

                def step(pair, n):
                    m = pair * 2 + n
                    rows = LAST if isinstance(pair, int) and n == NT - 1 else P
                    if not isinstance(pair, int) or n < NT:
                        for half in range(2):
                            wait(act, gate_done, 2 * m + half + 1)
                            nc.scalar.activation(silu[0:rows, half, :], ps_g[half][0:rows, :], ACT.Silu).then_inc(silu_done, 1)
                            wait(act, inner_done, 2 * m + half + 1)
                            if half == 0:
                                wait(act, first_down, m - 1)
                                dst = h_hi[0:rows, n % 2, :]
                            else:
                                dst = k_hi[0:rows, bass.ds(m * C, C)]
                            nc.scalar.copy(dst, inner[0:rows, half, :]).then_inc(inner_rounded, 1)
                    if not isinstance(pair, int) or n + 2 < NT:
                        round_ffn(pair, n + 2)
                steps(act, step)
                for b in range(B):
                    act.wait_ge(down_done, b + 1)
                    wait(act, sum_done, b - 1)
                    nc.scalar.copy(y16[:, b % 2, :], ps_d[b % 4][:]).then_inc(y_done, 1)

            @block.vector
            def _(dve):
                def norm_moments(b):
                    dve.wait_ge(ld_x[b], 16)
                    nc.vector.bn_stats(stats[:, b, :], acc[:, b, :]).then_inc(stats_done, 1)
                    dve.wait_ge(stats_done, b + 1)
                    nc.vector.bn_aggr(moments[:, b, :], stats[:, b, :]).then_inc(moments_done, 1)
                    dve.wait_ge(moments_done, b + 1)
                    nc.vector.tensor_scalar(rstd[:, b, :], moments[:, b, 1:2], EPS, None, ALU.add).then_inc(var_done, 1)

                def norm_apply(b):
                    dve.wait_ge(rstd_done, b + 1)
                    wait(dve, x_lo, b)
                    nc.vector.tensor_scalar(xn[:, 0, :], acc[:, b, :], moments[:, b, 0:1], rstd[:, b, :],
                                            ALU.subtract, ALU.mult).then_inc(xn_done, 1)

                norm_moments(0)
                norm_apply(0)
                dve.wait_ge(ld_mask, 16)
                nc.vector.tensor_copy(mask_f[:], mask_bytes[:].bitcast(U8)).then_inc(mask_step, 1)
                dve.wait_ge(mask_step, 1)
                nc.vector.reduce_sum(seen[:], mask_f[:], AX_X).then_inc(mask_step, 1)
                dve.wait_ge(mask_step, 2)
                nc.vector.tensor_scalar(live[:], seen[:], 1.0, None, ALU.min).then_inc(mask_step, 1)
                dve.wait_ge(mask_step, 3)
                nc.vector.tensor_scalar(dead[:], live[:], -1.0, 1.0, ALU.mult, ALU.add).then_inc(mask_step, 1)
                dve.wait_ge(mask_step, 4)
                nc.vector.tensor_scalar(keep[:], mask_f[:], dead[:], None, ALU.max).then_inc(mask_step, 1)
                for bank, hi, lo, rounded, done in ((ps_x, xT_hi, xT_lo, x_hi, x_lo), (ps_o, cT_hi, cT_lo, ctx_hi, ctx_lo)):
                    dve.wait_ge(rounded, 1)
                    nc.vector.tensor_tensor(lo[:, 0, :, :].rearrange("p k t -> p (k t)"), bank[:],
                                            hi[:, 0, :, :].rearrange("p k t -> p (k t)").bitcast(F32),
                                            ALU.subtract).then_inc(done, 1)
                for k in range(KT):
                    dve.wait_ge(wq0_rounded, k + 1)
                    nc.vector.tensor_tensor(wq_lo[0][:, k, :], wq_raw[:, k, :], wq_hi[0][:, k, :].bitcast(F32),
                                            ALU.subtract).then_inc(wq0_split, 1)
                dve.wait_ge(ld_tab, 16)
                nc.vector.tensor_scalar(q_tab[:], cs_tab[:], live[:], None, ALU.mult).then_inc(mask_step, 1)
                norm_moments(1)
                norm_apply(1)
                norm_moments(2)
                dve.wait_ge(keep_T, 1)
                nc.vector.tensor_copy(keepT[:], ps_pv[:, 0:T]).then_inc(tab_done, 1)
                dve.wait_ge(mask_step, 6)
                dve.wait_ge(tg_done, 1)

                def rope_products(xs, cs, sn, tab, mul):
                    heads = xs.shape[1]
                    def t(i, lo, hi):
                        return tab[:, i, lo:hi].unsqueeze(1).to_broadcast([P, heads, hi - lo])
                    h = D // 2
                    nc.vector.tensor_tensor(cs, xs, t(0, 0, D), ALU.mult)
                    nc.vector.tensor_tensor(sn[:, :, 0:h], xs[:, :, h:D], t(1, 0, h), ALU.mult)
                    nc.vector.tensor_tensor(sn[:, :, h:D], xs[:, :, 0:h], t(1, h, D), ALU.mult).then_inc(mul, 1)

                def unpack(pair, n, parts=range(4)):
                    m, par = pair * 2 + n, n % 2
                    q = packed[:, par].rearrange("p i c -> p (i c)")
                    if 0 in parts:
                        wait(dve, ld_q[par], (pair + n // 2 + 1) * (Q_LOADS * 16))
                        nc.vector.tensor_scalar(q, q, nib[:, 0:1], 15, ALU.logical_shift_right,
                                                ALU.bitwise_and).then_inc(unpacked, 1)
                    if 1 in parts:
                        zx = zero_x[:].rearrange("p (w e) -> p w e", e=PACK)
                        wait(dve, ld_zs[par], (pair + n // 2 + 1) * (ZS_LOADS * 16))
                        wait(dve, centred, m)
                        nc.vector.tensor_tensor(zx, zeros[:, par, :].unsqueeze(2).to_broadcast([P, 3 * WORDS, PACK]),
                                                nib[:, 1:1 + PACK].unsqueeze(1).to_broadcast([P, 3 * WORDS, PACK]),
                                                ALU.logical_shift_right).then_inc(zero_shifted, 1)
                    if 2 in parts:
                        wait(dve, zero_shifted, m + 1)
                        nc.vector.tensor_scalar(zero_x[:], zero_x[:], 15, None, ALU.bitwise_and).then_inc(zero_ready, 1)
                    if 3 in parts:
                        wait(dve, zero_ready, m + 1)
                        wait(dve, w_split, m - 1)
                        nc.vector.scalar_tensor_tensor(out=w_full[:, par].rearrange("p i c -> p (i c)"), in0=q, scalar=1.0,
                                                       in1=zero_x[:], op0=ALU.subtract,
                                                       op1=ALU.subtract).then_inc(centred, 1)

                def moments2_of(b):
                    dve.wait_ge(acc_done, TAIL + b + 1)
                    nc.vector.bn_stats(stats[:, b, :], acc[:, b, :]).then_inc(stats2, 1)
                    dve.wait_ge(stats2, b + 1)
                    nc.vector.bn_aggr(moments[:, b, :], stats[:, b, :]).then_inc(moments2, 1)
                    dve.wait_ge(moments2, b + 1)
                    nc.vector.tensor_scalar(rstd[:, b, :], moments[:, b, 1:2], EPS, None, ALU.add).then_inc(var2, 1)

                def norm2_apply(b):
                    dve.wait_ge(rstd2, b + 1)
                    wait(dve, prep2_T, b - 1)
                    nc.vector.tensor_scalar(xn[:, b % 2, :], acc[:, b, :], moments[:, b, 0:1], rstd[:, b, :],
                                            ALU.subtract, ALU.mult).then_inc(xn2, 1)

                def norm2_lo(b):
                    dve.wait_ge(prep2_hi, b + 1)
                    nc.vector.tensor_tensor(xT_lo[:, b, :, :].rearrange("p k t -> p (k t)"), norm2_bank(b),
                                            xT_hi[:, b, :, :].rearrange("p k t -> p (k t)").bitcast(F32),
                                            ALU.subtract).then_inc(prep2_lo, 1)

                def slot(base, group, s):
                    j = base + s
                    if 1 <= s < B - 2:
                        norm_apply(s + 2)
                    if runs(s - 1):
                        wait(dve, qk_rounded, j)
                        nc.vector.tensor_tensor(qT_lo[:], ps_qT[:], qT_hi[:].bitcast(F32), ALU.subtract)
                        nc.vector.tensor_tensor(kT_lo[:], ps_kv[:, 2, :], kT_hi[:].bitcast(F32),
                                                ALU.subtract).then_inc(qk_split, 1)
                    if s >= TAIL + 5:
                        norm2_apply(s - TAIL - 5)
                    if runs(s - 2) and not TAIL <= s < SLOTS:
                        par = (s - 2) % 2
                        wait(dve, p_rounded, j - 1)
                        nc.vector.tensor_tensor(p_lo[:], probs[:, par, :], p_hi[:].bitcast(F32),
                                                ALU.subtract).then_inc(p_split, 1)
                    if runs(s):
                        wait(dve, q_done, j + 1)
                        wait(dve, q_roped, j)
                        rope_products(ps_q, q_cos[:], q_sin[:], q_tab, q_mul)
                        if s < DVE_ADDS:
                            dve.wait_ge(q_mul, s + 1)
                            wait(dve, tr_done, s)
                            nc.vector.tensor_tensor(roped[:, 0:HG, :], q_cos[:], q_sin[:], ALU.add).then_inc(q_roped, 1)
                        if s == 0:
                            norm_apply(2)
                        wait(dve, v_rounded, j + 1)
                        nc.vector.tensor_tensor(v_lo[:, s % 4, :], ps_kv[:, 1, :], v_hi[:, s % 4, :].bitcast(F32),
                                                ALU.subtract).then_inc(v_split, 1)
                        rope_products(ps_kv[:, 0:1, :], k_cos[:].unsqueeze(1), k_sin[:].unsqueeze(1), cs_tab, k_mul)
                        wait(dve, k_mul, j + 1)
                        wait(dve, tr_done, j)
                        nc.vector.tensor_tensor(roped[:, HG, :], k_cos[:], k_sin[:], ALU.add).then_inc(k_roped, 1)
                    if TAIL + 5 <= s < TAIL + 8:
                        norm2_lo(s - TAIL - 5)
                    if s == TAIL + 10:
                        norm2_lo(5)
                    if s >= TAIL + 4:
                        moments2_of(s - TAIL - 4)
                    if s == TAIL + 8:
                        unpack(0, 1, (3,))
                    if s == TAIL + 10:
                        norm2_apply(6)
                    if runs(s - 2):
                        wait(dve, tot_done, j - 1)
                        wait(dve, norm_done, j - 2)
                        nc.vector.reciprocal(r_tot[:], ps_tot[:]).then_inc(inverted, 1)
                        wait(dve, inverted, j - 1)
                        wait(dve, pv_done, j - 1)
                        wait(dve, a_split, j - 2)
                        nc.vector.tensor_tensor(attn[:], ps_pv[:], r_tot[:], ALU.mult).then_inc(norm_done, 1)
                    if TAIL + 8 <= s < TAIL + 10:
                        norm2_lo(s - TAIL - 5)
                    if s == TAIL:
                        dve.wait_ge(ld_nib, 16)
                        unpack(0, 0, (0,))
                        unpack(0, 1, (0,))
                        dve.wait_ge(q_done, TAIL)
                        dve.wait_ge(kv_done, TAIL)
                    if TAIL + 1 <= s < TAIL + 4:
                        unpack(0, 0, (s - TAIL,))
                    if TAIL + 4 <= s < TAIL + 6:
                        unpack(0, 1, (s - TAIL - 3,))
                    if runs(s - 3) and not TAIL <= s < SLOTS + 2:
                        b = (s - 3) % B
                        wait(dve, o_done, j - 2)
                        wait(dve, acc_done, j - 3)
                        nc.vector.scalar_tensor_tensor(out=acc[:, b, :], in0=ps_o[:], scalar=tgates[:, 0:1],
                                                       in1=acc[:, b, :], op0=ALU.mult,
                                                       op1=ALU.add).then_inc(acc_done, 1)
                    if s + 3 < B:
                        norm_moments(s + 3)
                    if s == TAIL + 10:
                        moments2_of(7)
                        norm2_lo(6)
                all_slots(dve, slot)
                norm2_apply(7)
                norm2_lo(7)

                def step(pair, n):
                    m = pair * 2 + n
                    rows = LAST if isinstance(pair, int) and n == NT - 1 else P
                    if not isinstance(pair, int) or n + 2 < NT:
                        unpack(pair, n + 2)
                    if not isinstance(pair, int) or n < NT:
                        for half in range(2):
                            wait(dve, silu_done, 2 * m + half + 1)
                            wait(dve, up_done, 2 * m + half + 1)
                            wait(dve, inner_split, 2 * m + half - 1)
                            nc.vector.tensor_tensor(inner[0:rows, half, :], ps_u[half][0:rows, :], silu[0:rows, half, :],
                                                    ALU.mult).then_inc(inner_done, 1)
                            wait(dve, inner_rounded, 2 * m + half + 1)
                            if half == 0:
                                lo, hi = h_lo[0:rows, n % 2, :], h_hi[0:rows, n % 2, :]
                            else:
                                lo, hi = k_lo[0:rows, bass.ds(m * C, C)], k_hi[0:rows, bass.ds(m * C, C)]
                            nc.vector.tensor_tensor(lo, inner[0:rows, half, :], hi.bitcast(F32),
                                                    ALU.subtract).then_inc(inner_split, 1)
                steps(dve, step)
                for b in range(B):
                    dve.wait_ge(y_done, b + 1)
                    nc.vector.scalar_tensor_tensor(out=acc[:, b, :], in0=y16[:, b % 2, :], scalar=tgates[:, 1:2],
                                                   in1=acc[:, b, :], op0=ALU.mult, op1=ALU.add).then_inc(sum_done, 1)

            @block.tensor
            def _(pe):
                pe.wait_ge(id_done, 1)

                def prep(b):
                    pe.wait_ge(xn_done, b + 1)
                    wait(pe, x_lo, b)
                    for i in range(KT):
                        mm = nc.tensor.transpose(ps_x[:, i * T:(i + 1) * T], xn[:, 0, i * P:(i + 1) * P], ident[:])
                    mm.then_inc(x_T, 1)
                    i = raw_of(b)
                    pe.wait_ge(ld_ctx[i], 16 if b < 2 else b // 2 * 16)
                    wait(pe, ctx_lo, b)
                    wait(pe, acc_done, b - 5)
                    for k in range(KT):
                        mm = nc.tensor.transpose(ps_o[:, k * T:(k + 1) * T], ctx_raw[i][:, k * P:(k + 1) * P], ident[:])
                    mm.then_inc(ctx_T, 1)

                prep(0)
                pe.wait_ge(mask_step, 5)
                nc.tensor.transpose(ps_pv[:, 0:T], keep[:], ident[:]).then_inc(keep_T, 1)

                def gate_up(pair, n, half, i):
                    m, par = pair * 2 + n, n % 2
                    cols = LAST if isinstance(pair, int) and n == NT - 1 else P
                    bank, free, done = ((ps_g[half], silu_done, gate_done), (ps_u[half], inner_done, up_done))[i]
                    seqs = slice(half * HALF, (half + 1) * HALF)
                    wait(pe, free, 2 * m + half - 1)
                    for k in range(KT):
                        mm = split_matmul(nc, bank[0:cols, :].rearrange("p (b t) -> p b t", b=HALF),
                                          gu_hi[:, par, i, k, 0:cols], gu_lo[:, par, i, k, 0:cols],
                                          xT_hi[:, seqs, k, :], xT_lo[:, seqs, k, :], k == 0, k == KT - 1)
                    mm.then_inc(done, 1)

                def step(pair, n):
                    wait(pe, w_split, pair * 2 + n + 1)
                    for half in range(2):
                        for i in range(2):
                            gate_up(pair, n, half, i)

                def norm2_T(b):
                    pe.wait_ge(xn2, b + 1)
                    if b < B - 2:
                        wait(pe, prep2_lo, b)
                    for i in range(KT):
                        mm = nc.tensor.transpose(norm2_bank(b)[:, i * T:(i + 1) * T], xn[:, b % 2, i * P:(i + 1) * P], ident[:])
                    mm.then_inc(prep2_T, 1)

                def down_first(pair, n, start):
                    m, par = pair * 2 + n, n % 2
                    rows = LAST if isinstance(pair, int) and n == NT - 1 else P
                    last = isinstance(pair, int) and n == NT - 1
                    wait(pe, inner_split, 2 * m + 1)
                    for b in range(HALF):
                        mm = split_matmul(nc, ps_d[b][:], h_hi[0:rows, par, b * T:(b + 1) * T],
                                          h_lo[0:rows, par, b * T:(b + 1) * T],
                                          wd_hi[0:rows, bass.ds(m * C, C)], wd_lo[0:rows, bass.ds(m * C, C)], start, last)
                        if last:
                            mm.then_inc(down_done, 1)
                    return mm

                pe.wait_ge(ones_done, 1)

                def slot(base, group, s):
                    j = base + s
                    g = group + s // B
                    wpar = (s // B) % 2
                    if runs(s - 1):
                        wait(pe, q_roped, j)
                        wait(pe, k_roped, j)
                        wait(pe, qk_split, j - 1)
                        wait(pe, v_split, j)
                        for h in range(HG):
                            nc.tensor.transpose(ps_qT[:, h * T:(h + 1) * T], roped[:, h, :], ident[:])
                        nc.tensor.transpose(ps_kv[:, 2, :], roped[:, HG, :], ident[:]).then_inc(tr_done, 1)
                    if runs(s):
                        b = s % B
                        if s < B:
                            pe.wait_ge(x_lo, b + 1)
                        elif b == 0:
                            wait(pe, wq_split, g * KT)
                        for k in range(KT):
                            if s == 0:
                                pe.wait_ge(wq0_split, k + 1)
                            mm = split_matmul(nc, ps_q[:].rearrange("p h d -> p (h d)"),
                                              xT_hi[:, b, k, :], xT_lo[:, b, k, :],
                                              wq_hi[wpar][:, k, :], wq_lo[wpar][:, k, :], k == 0, k == KT - 1)
                        mm.then_inc(q_done, 1)
                        if s == 0:
                            prep(1)
                            pe.wait_ge(wkv0_split, 1)
                        elif s + 2 < B:
                            prep(s + 2)
                        if s >= TAIL + 5:
                            norm2_T(s - TAIL - 5)
                        if s < B:
                            pe.wait_ge(ctx_lo, b + 1)
                        wait(pe, qk_split, j)
                        for k in range(KT):
                            mm = split_matmul(nc, ps_kv[:, 0:2, :].rearrange("p h d -> p (h d)"),
                                              cT_hi[:, b, k, :], cT_lo[:, b, k, :],
                                              wkv_hi[wpar][:, k, :], wkv_lo[wpar][:, k, :], k == 0, k == KT - 1)
                        mm.then_inc(kv_done, 1)
                        if s == 0:
                            prep(2)
                    if runs(s - 1):
                        wait(pe, qk_split, j)
                        wait(pe, tanh_done, j - 1)
                        split_matmul(nc, ps_s[:], kT_hi[:], kT_lo[:],
                                     qT_hi[:], qT_lo[:], True, True).then_inc(s_done, 1)
                    if s == TAIL + 9:
                        pe.wait_ge(w_split, 1)
                        pe.wait_ge(prep2_lo, HALF)
                        pe.wait_ge(q_roped, SLOTS)
                        gate_up(0, 0, 0, 0)
                    if runs(s - 2):
                        vb = (s - 2) % 4
                        wait(pe, p_split, j - 1)
                        wait(pe, norm_done, j - 2)
                        if s == 2:
                            pe.wait_ge(tab_done, 1)
                        nc.tensor.matmul(ps_tot[:], ones[:], p_hi[:], start=True, stop=False)
                        nc.tensor.matmul(ps_tot[:], ones[:], p_lo[:], start=False, stop=True).then_inc(tot_done, 1)
                        mm = split_matmul(nc, ps_pv[:], v_hi[:, vb, :], v_lo[:, vb, :], p_hi[:], p_lo[:], True, True)
                        mm.then_inc(pv_done, 1)
                    if s == TAIL + 10:
                        pe.wait_ge(qk_split, SLOTS)
                        gate_up(0, 0, 0, 1)
                    if s >= TAIL + 8:
                        norm2_T(s - TAIL - 5)
                    if runs(s - 3):
                        wp = ((s - 3) // B) % 2
                        if (s - 3) % B == 0:
                            wait(pe, wo_split, (group + (s - 3) // B + 1) * HG)
                        wait(pe, a_split, j - 2)
                        wait(pe, acc_done, j - 3)
                        if s < B:
                            pe.wait_ge(ctx_hi, min(s + 3, B))
                        for h in range(HG):
                            mm = split_matmul(nc, ps_o[:], aT_hi[:, h * T:(h + 1) * T],
                                              aT_lo[:, h * T:(h + 1) * T],
                                              wo_hi[wp][:, h, :], wo_lo[wp][:, h, :], h == 0, h == HG - 1)
                        mm.then_inc(o_done, 1)
                    if s == TAIL + 10:
                        pe.wait_ge(norm_done, SLOTS)
                        norm2_T(6)
                all_slots(pe, slot)
                norm2_T(7)
                pe.wait_ge(prep2_lo, B)
                gate_up(0, 0, 1, 0)
                gate_up(0, 0, 1, 1)
                step(0, 1)
                down_first(0, 0, True).then_inc(first_down, 1)
                with pe.Fori(0, 4) as i:
                    for n in range(2):
                        step(i, n + 2)
                        down_first(i, n + 1, False).then_inc(first_down, 1)
                step(0, NT - 1)
                down_first(0, NT - 2, False).then_inc(first_down, 1)
                down_first(0, NT - 1, False)
                for b in range(HALF, B):
                    pe.wait_ge(inner_split, 2 * NT)
                    pe.wait_ge(y_done, b - HALF + 1)
                    for n in range(NT):
                        rows = LAST if n == NT - 1 else P
                        at = n * C + (b - HALF) * T
                        mm = split_matmul(nc, ps_d[b % 4][:], k_hi[0:rows, at:at + T], k_lo[0:rows, at:at + T],
                                          wd_hi[0:rows, n * C:(n + 1) * C], wd_lo[0:rows, n * C:(n + 1) * C],
                                          n == 0, n == NT - 1)
                    mm.then_inc(down_done, 1)


_OUT = ((B, T, C), "float32")


def rope_tables():
    exponents = np.arange(0, D, 2, dtype=np.float32)
    inv_freq = (np.float32(1.0) / np.float32(10000.0) ** (exponents / np.float32(D))).astype(np.float32)
    phase = np.arange(T, dtype=np.float32)[:, None] * inv_freq[None, :]
    phase = np.concatenate([phase, phase], axis=1).astype(np.float32)
    sign = np.where(np.arange(D) < D // 2, -1.0, 1.0).astype(np.float32)
    return np.stack([np.cos(phase), np.sin(phase) * sign], axis=1).astype(np.float32)


def nibble_table():
    rows = np.arange(P)[:, None] % PACK * 4
    return np.concatenate([rows, np.tile(np.arange(PACK) * 4, (P, 1))], axis=1).astype(np.uint32)


def kernel(x, ctx_4096, mask_1x1xSxS2_bk0, g_xattn, g_ffn, L0_xattn_Wq, L0_xattn_Wk, L0_xattn_Wv, L0_xattn_Wo,
           L0_ffn_gate_qweight, L0_ffn_gate_scales, L0_ffn_gate_zeros, L0_ffn_up_qweight, L0_ffn_up_scales,
           L0_ffn_up_zeros, L0_ffn_down_qweight, L0_ffn_down_scales, L0_ffn_down_zeros):
    import concourse.bacc as bacc
    from concourse.bass_utils import run_bass_kernel_spmd

    def bits(a):
        return np.ascontiguousarray(a).view(np.uint32)

    ins = [("x", np.ascontiguousarray(x)), ("ctx", np.ascontiguousarray(ctx_4096)),
           ("mask", np.ascontiguousarray(mask_1x1xSxS2_bk0).reshape(T, T).view(np.uint32)),
           ("g_xattn", np.ascontiguousarray(g_xattn)), ("g_ffn", np.ascontiguousarray(g_ffn)),
           ("Wq", np.ascontiguousarray(L0_xattn_Wq)), ("Wk", np.ascontiguousarray(L0_xattn_Wk)),
           ("Wv", np.ascontiguousarray(L0_xattn_Wv)), ("Wo", np.ascontiguousarray(L0_xattn_Wo)),
           ("gate_q", bits(L0_ffn_gate_qweight)), ("gate_s", np.ascontiguousarray(L0_ffn_gate_scales)),
           ("gate_z", bits(L0_ffn_gate_zeros)),
           ("up_q", bits(L0_ffn_up_qweight)), ("up_s", np.ascontiguousarray(L0_ffn_up_scales)),
           ("up_z", bits(L0_ffn_up_zeros)),
           ("down_q", bits(L0_ffn_down_qweight)), ("down_s", np.ascontiguousarray(L0_ffn_down_scales)),
           ("down_z", bits(L0_ffn_down_zeros)),
           ("cos_sin", rope_tables()), ("nibble", nibble_table())]
    nc = bacc.Bacc("TRN2", target_bir_lowering=False, num_devices=1, dynamic_dma_scratch_size=256)
    arrays, args = {}, []
    for name, a in ins:
        arrays[f"in_{name}"] = a
        args.append(nc.dram_tensor(f"in_{name}", a.shape, mybir.dt.from_np(a.dtype), kind="ExternalInput").ap())
    args.append(nc.dram_tensor("out_dram", _OUT[0], F32, kind="ExternalOutput").ap())
    flamingo_block(nc, *args)
    r = run_bass_kernel_spmd(nc, [arrays], core_ids=[0])
    return r.results[0]["out_dram"]
```

```python
from contextlib import ExitStack

import numpy as np

import concourse.bass as bass
from concourse import mybir

ALU = mybir.AluOpType
ACT = mybir.ActivationFunctionType
F32 = mybir.dt.float32
F32R = mybir.dt.float32r
F16 = mybir.dt.float16
U32 = mybir.dt.uint32
U8 = mybir.dt.uint8
AX_X = mybir.AxisListType.X

P = 128
B = 8
T = 128
C = 512
KT = C // P
KV = 8
HG = 4
D = 128
GC = HG * D
SLOTS = KV * B
LOOPED = 16
INTER = 1376
NT = 11
LAST = INTER - (NT - 1) * P
PACK = 8
WORDS = C // PACK
HALF = B // 2
ATTN_MULT = 0.08838834764831845
MAX_ATTN = 30.0
EPS = 1e-5
DVE_ADDS = 3
BYTES = {F32: 4, F32R: 4, U32: 4, F16: 2}
SBUF_BASE = 384
TAIL = SLOTS - B


def wait(eng, s, n):
    if not isinstance(n, int) or n > 0:
        eng.wait_ge(s, n)


def split_matmul(nc, out, w_hi, w_lo, m_hi, m_lo, first, last):
    nc.tensor.matmul(out, w_hi, m_hi, start=first, stop=False)
    nc.tensor.matmul(out, w_hi, m_lo, start=False, stop=False)
    return nc.tensor.matmul(out, w_lo, m_hi, start=False, stop=last)


def flamingo_block(nc, x, ctx_in, mask, g_xattn, g_ffn, Wq, Wk, Wv, Wo,
                   gate_q, gate_s, gate_z, up_q, up_s, up_z, down_q, down_s, down_z,
                   cos_sin, nibble, out):
    with ExitStack() as here:
        at = [SBUF_BASE]

        def over(name, shape, dt, offset):
            return nc.alloc_sbuf_tensor_at(name, shape, dt, offset=offset)

        def sb(name, shape, dt):
            offset = at[0]
            at[0] += (int(np.prod(shape[1:])) * BYTES[dt] + 31) // 32 * 32
            return over(name, shape, dt, offset)

        def ps(name, shape):
            return here.enter_context(nc.psum_tensor(name, shape, F32))

        def sem(name):
            return here.enter_context(nc.semaphore(name))

        acc = sb("acc", [P, B, C], F32)
        xT_hi = sb("xT_hi", [P, B, KT, T], F32R)
        xT_lo = sb("xT_lo", [P, B, KT, T], F32R)
        xn = sb("xn", [P, 2, C], F32)
        stats = sb("stats", [P, B, 6], F32)
        moments = sb("moments", [P, B, 2], F32)
        rstd = sb("rstd", [P, B, 1], F32)
        minus_half = sb("minus_half", [P, 1], F32)
        ident = sb("ident", [P, P], F32)
        gates = sb("gates", [P, 2], F32)
        tgates = sb("tgates", [P, 2], F32)
        table_load = sb("table_load", [P, 1], F32)
        nib = sb("nib", [P, 1 + PACK], U32)

        raw_at = at[0]
        wq_raw = sb("wq_raw", [P, KT, GC], F32)
        wkv_raw = sb("wkv_raw", [P, KT, 2 * D], F32)
        wo_raw_at = at[0]
        wo_raw = sb("wo_raw", [P, HG, C], F32)
        wq_hi, wq_lo, wkv_hi, wkv_lo, wo_hi, wo_lo = [], [], [], [], [], []
        qkv_at, wo_at = [], []

        def place_weights(par):
            qkv_at.append(at[0])
            wq_hi.append(sb(f"wq_hi{par}", [P, KT, GC], F32R))
            wq_lo.append(sb(f"wq_lo{par}", [P, KT, GC], F32R))
            wkv_hi.append(sb(f"wkv_hi{par}", [P, KT, 2 * D], F32R))
            wkv_lo.append(sb(f"wkv_lo{par}", [P, KT, 2 * D], F32R))
            wo_at.append(at[0])
            wo_hi.append(sb(f"wo_hi{par}", [P, HG, C], F32R))
            wo_lo.append(sb(f"wo_lo{par}", [P, HG, C], F32R))

        place_weights(0)
        cT_hi_at = at[0]
        cT_hi = sb("cT_hi", [P, B, KT, T], F32R)
        q_cos = sb("q_cos", [P, HG, D], F32)
        q_sin = sb("q_sin", [P, HG, D], F32)
        capped = sb("capped", [P, GC], F32)
        cT_lo_at = at[0]
        cT_lo = sb("cT_lo", [P, B, KT, T], F32R)
        p_hi = sb("p_hi", [P, GC], F32R)
        p_lo = sb("p_lo", [P, GC], F32R)
        attn = sb("attn", [P, GC], F32)
        place_weights(1)
        small_at = at[0]
        probs = sb("probs", [P, 2, GC], F32)
        roped = sb("roped", [P, HG + 1, D], F32)
        qT_hi = sb("qT_hi", [P, GC], F32R)
        qT_lo = sb("qT_lo", [P, GC], F32R)
        kT_hi = sb("kT_hi", [P, T], F32R)
        kT_lo = sb("kT_lo", [P, T], F32R)
        v_hi = sb("v_hi", [P, 4, D], F32R)
        v_lo = sb("v_lo", [P, 4, D], F32R)
        aT_hi = sb("aT_hi", [P, GC], F32R)
        aT_lo = sb("aT_lo", [P, GC], F32R)
        k_cos = sb("k_cos", [P, D], F32)
        k_sin = sb("k_sin", [P, D], F32)
        cs_tab = sb("cs_tab", [P, 2, D], F32)
        q_tab = sb("q_tab", [P, 2, D], F32)
        mask_bytes = sb("mask_bytes", [P, T // 4], U32)
        mask_f = sb("mask_f", [P, T], F32)
        keep = mask_f
        keepT = sb("keepT", [P, T], F32)
        seen = sb("seen", [P, 1], F32)
        live = sb("live", [P, 1], F32)
        dead = sb("dead", [P, 1], F32)
        ones = sb("ones", [P, P], F32R)
        r_tot = sb("r_tot", [P, GC], F32)
        ctx_rows = over("ctx_rows", [P, C], F32, wo_at[1] + (2 * HG - 1) * C * 4)
        ctx_raw = [capped[:], attn[:], ctx_rows[:], xn[:, 1, :]]

        packed = over("packed", [P, 2, 3, C], U32, raw_at)
        zeros = over("zeros", [P, 2, 3 * WORDS], U32, wo_raw_at)
        scales = over("scales", [P, 2, 2, C], F16, wo_raw_at + 6 * WORDS * 4)
        gate_s16 = over("gate_s16", [P, NT, KT], F16, wo_raw_at + 11 * C)
        gate_s32 = over("gate_s32", [P, 2, KT], F32, wo_raw_at + 11 * C + 128)
        zero_x = over("zero_x", [P, 3 * C], U32, qkv_at[0])
        w_full = over("w_full", [P, 2, 2, C], F32, qkv_at[0] + 3 * C * 4)
        later_sum = over("later_sum", [P, 2, C], F32, qkv_at[0] + 7 * C * 4)
        gate_sum = over("gate_sum", [P, 2, C], F32, qkv_at[0] + 10 * C * 4)
        gate_int = over("gate_int", [P, 2, KT, P], F32R, wo_at[0])
        up_hi = over("up_hi", [P, 2, KT, P], F32R, wo_at[0] + 2 * C * 4)
        up_lo = over("up_lo", [P, 2, KT, P], F32R, wo_at[0] + 4 * C * 4)
        first_sum = over("first_sum", [P, 2, C], F32, wo_at[0] + 6 * C * 4)
        wd_hi = over("wd_hi", [P, NT * C], F32R, cT_hi_at)
        wd_lo = over("wd_lo", [P, NT * C], F32R, cT_lo_at)
        silu = over("silu", [P, 2, C], F32, qkv_at[1])
        inner = over("inner", [P, 2, C], F32, qkv_at[1] + 2 * C * 4)
        h_hi = over("h_hi", [P, 2, C], F32R, qkv_at[1] + 4 * C * 4)
        h_lo = over("h_lo", [P, 2, C], F32R, qkv_at[1] + 6 * C * 4)
        y16 = over("y16", [P, 2, C], F16, qkv_at[1] + 8 * C * 4)
        share = over("share", [P, C], F32, qkv_at[0] + 9 * C * 4)
        k_hi = over("k_hi", [P, NT * C], F32R, qkv_at[1] + 9 * C * 4)
        k_lo = over("k_lo", [P, NT * C], F32R, small_at)

        bank_q = ps("bank_q", [P, C])
        bank_kv = ps("bank_kv", [P, C])
        ps_q = bank_q[:].rearrange("p (h d) -> p h d", h=HG)
        ps_qT = ps("ps_qT", [P, GC])
        ps_s = ps("ps_s", [P, GC])
        ps_pv = ps("ps_pv", [P, GC])
        ps_tot = ps("ps_tot", [P, GC])
        ps_x = ps("ps_x", [P, C])
        kv_banks = [bank[:].rearrange("p (h d) -> p h d", h=4) for bank in (bank_kv, ps_x)]

        def kv_bank(s):
            return kv_banks[s % 2 if B - 1 <= s < TAIL + 4 else 0]

        ps_o = ps("ps_o", [P, C])
        ps_g = [bank_q[:], ps_qT[:]]
        ps_u = [bank_kv[:], ps_s[:]]
        ps_d = [ps_pv[:], ps_tot[:], ps_x[:], ps_o[:]]

        def norm2_bank(b):
            return ps_d[2] if b < B - 2 else ps_d[b - (B - 2)]

        ld_x = [sem(f"ld_x{b}") for b in range(B)]
        ld_ctx = [sem(f"ld_ctx{i}") for i in range(4)]
        ld_tab, ld_mask, ld_gates = sem("ld_tab"), sem("ld_mask"), sem("ld_gates")
        ld_wq, ld_wkv, ld_wo = sem("ld_wq"), sem("ld_wkv"), sem("ld_wo")
        id_zero, id_done, ones_done, half_done = sem("id_zero"), sem("id_done"), sem("ones_done"), sem("half_done")
        stats_done, moments_done, var_done = sem("stats_done"), sem("moments_done"), sem("var_done")
        rstd_done, xn_done = sem("rstd_done"), sem("xn_done")
        x_T, x_hi, x_lo = sem("x_T"), sem("x_hi"), sem("x_lo")
        ctx_T, ctx_hi, ctx_lo = sem("ctx_T"), sem("ctx_hi"), sem("ctx_lo")
        ld_wq0 = [sem("ld_wq0_a"), sem("ld_wq0_b")]
        wq0_rounded, wq0_split, wkv0_rounded, wkv0_split = (sem("wq0_rounded"), sem("wq0_split"),
                                                            sem("wkv0_rounded"), sem("wkv0_split"))
        mask_step, keep_T, tab_done, tg_done = sem("mask_step"), sem("keep_T"), sem("tab_done"), sem("tg_done")
        wq_rounded, wq_split = sem("wq_rounded"), sem("wq_split")
        wo_rounded, wo_split = sem("wo_rounded"), sem("wo_split")
        q_done, kv_done, tr_done = sem("q_done"), sem("kv_done"), sem("tr_done")
        q_mul, k_mul, q_roped, k_roped = sem("q_mul"), sem("k_mul"), sem("q_roped"), sem("k_roped")
        qk_rounded, qk_split, v_rounded, v_split = sem("qk_rounded"), sem("qk_split"), sem("v_rounded"), sem("v_split")
        s_done, tanh_done, exp_done, masked = sem("s_done"), sem("tanh_done"), sem("exp_done"), sem("masked")
        p_rounded, p_split, pv_done = sem("p_rounded"), sem("p_split"), sem("pv_done")
        tot_done, inverted, norm_done = sem("tot_done"), sem("inverted"), sem("norm_done")
        a_rounded, a_split, o_done, acc_done = sem("a_rounded"), sem("a_split"), sem("o_done"), sem("acc_done")

        share_scaled = sem("share_scaled")
        ld_nib, ld_q, ld_zs = sem("ld_nib"), [sem("ld_q0"), sem("ld_q1")], [sem("ld_zs0"), sem("ld_zs1")]
        stats2, moments2, var2, rstd2, xn2 = sem("stats2"), sem("moments2"), sem("var2"), sem("rstd2"), sem("xn2")
        prep2_T, prep2_hi, prep2_lo = sem("prep2_T"), sem("prep2_hi"), sem("prep2_lo")
        unpacked, zero_shifted, zero_ready, centred = sem("unpacked"), sem("zero_shifted"), sem("zero_ready"), sem("centred")
        scaled, w_rounded, w_split = sem("scaled"), sem("w_rounded"), sem("w_split")
        ld_gate_s, gate_s_done = sem("ld_gate_s"), sem("gate_s_done")
        group_done, even_scaled, odd_scaled, gate_summed = (sem("group_done"), sem("even_scaled"), sem("odd_scaled"),
                                                            sem("gate_summed"))
        gate_centred = sem("gate_centred")
        up_done, silu_done, inner_done = sem("up_done"), sem("silu_done"), sem("inner_done")
        inner_rounded, inner_split = sem("inner_rounded"), sem("inner_split")
        first_down, down_done, y_done, sum_done, stored = (sem("first_down"), sem("down_done"), sem("y_done"),
                                                           sem("sum_done"), sem("stored"))
        Q_LOADS, ZS_LOADS = 2 * KT + 1, 5

        def steps(eng, step):
            step(0, 0)
            step(0, 1)
            with eng.Fori(1, 4) as i:
                for n in range(2):
                    step(i, n)
            for n in range(8, NT + 1):
                step(0, n)

        early_parts = [[], [(0, 4), (0, 5)], [(0, 6), (0, 7)], [(1, 0), (1, 1)], [(1, 2)], [(1, 3), (1, 4)],
                       [(1, 5), (1, 6)], [(1, 7)]]

        def raw_of(b):
            return b if b < 2 else 2 + b % 2

        def all_slots(eng, slot):
            for s in range(B):
                slot(0, 0, s)
            with eng.Fori(0, (SLOTS - 2 * B) // LOOPED) as i:
                for s in range(B, B + LOOPED):
                    slot(i * LOOPED, i * (LOOPED // B), s)
            for s in range(SLOTS - B, SLOTS + 3):
                slot(0, 0, s)

        def runs(s):
            return 0 <= s < SLOTS

        wq_v = Wq.rearrange("(k p) n -> p k n", p=P)
        wk_v = Wk.rearrange("(k p) n -> p k n", p=P)
        wv_v = Wv.rearrange("(k p) n -> p k n", p=P)
        wo_v = Wo.rearrange("(h p) n -> p h n", p=P)

        with nc.Block() as block:

            @block.sync
            def _(sp):
                def load_wqkv(g):
                    wait(sp, wq_split, (g - 1) * KT)
                    sp.dma_start(wq_raw[:], wq_v[:, :, bass.ds(g * GC, GC)]).then_inc(ld_wq, 16)
                    sp.dma_start(wkv_raw[:, :, 0:D], wk_v[:, :, bass.ds(g * D, D)]).then_inc(ld_wkv, 16)
                    sp.dma_start(wkv_raw[:, :, D:2 * D], wv_v[:, :, bass.ds(g * D, D)]).then_inc(ld_wkv, 16)

                def load_wo(g):
                    wait(sp, wo_split, g * HG)
                    sp.dma_start(wo_raw[:], wo_v[:, bass.ds(g * HG, HG), :]).then_inc(ld_wo, 16)

                def load_ctx(b):
                    i = raw_of(b)
                    wait(sp, ctx_lo, b - 1 if b >= 4 else 0)
                    sp.dma_start(ctx_raw[i], ctx_in[b]).then_inc(ld_ctx[i], 16)

                def load_x(b):
                    sp.dma_start(acc[:, b, :], x[b]).then_inc(ld_x[b], 16)

                load_x(0)
                sp.dma_start(mask_bytes[:], mask).then_inc(ld_mask, 16)
                load_ctx(0)
                for i in range(2):
                    ks = slice(2 * i, 2 * i + 2)
                    sp.dma_start(wq_raw[:, ks, :], wq_v[:, ks, 0:GC]).then_inc(ld_wq0[i], 16)
                sp.dma_start(cs_tab[:], cos_sin).then_inc(ld_tab, 16)
                load_x(1)
                sp.dma_start(wkv_raw[:, :, 0:D], wk_v[:, :, 0:D]).then_inc(ld_wkv, 16)
                sp.dma_start(wkv_raw[:, :, D:2 * D], wv_v[:, :, 0:D]).then_inc(ld_wkv, 16)
                load_ctx(1)
                sp.dma_start(gates[:, 0:1], g_xattn.unsqueeze(0).to_broadcast([P, 1])).then_inc(ld_gates, 16)
                sp.dma_start(gates[:, 1:2], g_ffn.unsqueeze(0).to_broadcast([P, 1])).then_inc(ld_gates, 16)
                load_x(2)
                load_ctx(2)
                sp.dma_start(wo_raw[:], wo_v[:, 0:HG, :]).then_inc(ld_wo, 16)
                for b in range(3, B):
                    load_x(b)
                load_ctx(3)
                sp.wait_ge(wq0_split, KT)
                sp.wait_ge(wkv0_split, 1)
                sp.dma_start(nib[:], nibble).then_inc(ld_nib, 16)
                load_wqkv(1)
                load_ctx(4)
                load_ctx(5)
                load_wo(1)
                load_ctx(6)
                load_ctx(7)
                with sp.Fori(2, KV) as g:
                    load_wqkv(g)
                    load_wo(g)

                def load_q(pair, n):
                    m = pair * 2 + n
                    par = n % 2
                    cols, rows = (LAST, LAST) if isinstance(pair, int) and n == NT - 1 else (P, P)
                    wait(sp, scaled, m - 1)
                    for i, q in enumerate((gate_q, up_q)):
                        for k in range(KT):
                            src = q[k * 16:(k + 1) * 16, bass.ds(m * P, cols)].unsqueeze(1).to_broadcast([16, PACK, cols])
                            sp.dma_start(packed[:, par, i, k * P:k * P + cols], src).then_inc(ld_q[par], 16)
                    src = down_q[bass.ds(m * 16, rows // PACK), :].unsqueeze(1).to_broadcast([rows // PACK, PACK, C])
                    sp.dma_start(packed[0:rows, par, 2, :], src).then_inc(ld_q[par], 16)

                def load_zs(pair, n):
                    m = pair * 2 + n
                    par = n % 2
                    cols = LAST if isinstance(pair, int) and n == NT - 1 else P
                    for i, z in enumerate((gate_z, up_z)):
                        src = z[:, bass.ds(m * (P // PACK), cols // PACK)].unsqueeze(0).to_broadcast([P, KT, cols // PACK])
                        sp.dma_start(zeros[:, par, i * WORDS:(i + 1) * WORDS].rearrange("p (k w) -> p k w", k=KT)[:, :, 0:cols // PACK],
                                     src).then_inc(ld_zs[par], 16)
                    src = up_s[:, bass.ds(m * P, cols)].unsqueeze(0).to_broadcast([P, KT, cols])
                    sp.dma_start(scales[:, par, 0, :].rearrange("p (k c) -> p k c", k=KT)[:, :, 0:cols],
                                 src).then_inc(ld_zs[par], 16)
                    sp.dma_start(zeros[:, par, 2 * WORDS:3 * WORDS],
                                 down_z[bass.ds(m, 1), :].to_broadcast([P, WORDS])).then_inc(ld_zs[par], 16)
                    sp.dma_start(scales[:, par, 1, :],
                                 down_s[bass.ds(m, 1), :].to_broadcast([P, C])).then_inc(ld_zs[par], 16)

                sp.wait_ge(wq_split, (KV - 1) * KT)
                load_q(0, 0)
                load_q(0, 1)
                sp.wait_ge(wo_split, KV * HG)
                load_zs(0, 0)
                load_zs(0, 1)
                sp.dma_start(gate_s16[:], gate_s).then_inc(ld_gate_s, 16)
                with sp.Fori(1, 5) as i:
                    for n in range(2):
                        load_q(i, n)
                        load_zs(i, n)
                load_q(0, NT - 1)
                load_zs(0, NT - 1)
                for b in range(B):
                    sp.wait_ge(sum_done, b + 1)
                    sp.dma_start(out[b], acc[:, b, :]).then_inc(stored, 16)
                sp.wait_ge(stored, 16 * B)

            @block.gpsimd
            def _(pool):
                nc.gpsimd.memset(ident[:], 0.0).then_inc(id_zero, 1)
                nc.gpsimd.memset(minus_half[:], -0.5).then_inc(half_done, 1)
                pool.wait_ge(id_zero, 1)
                nc.gpsimd.affine_select(out=ident[:], in_=ident[:], compare_op=ALU.not_equal, fill=1.0,
                                        base=0, pattern=[[-1, P]], channel_multiplier=1).then_inc(id_done, 1)
                nc.gpsimd.memset(ones[:].bitcast(F32), 1.0).then_inc(ones_done, 1)
                pool.wait_ge(half_done, 1)

                def invert_std(b):
                    pool.wait_ge(var_done, b + 1)
                    nc.gpsimd.tensor_tensor(rstd[:, b, :], rstd[:, b, :], minus_half[:], ALU.pow).then_inc(rstd_done, 1)

                def prep(b):
                    for copied, hi, lo, rounded, done in ((xn[:, 0, :], xT_hi, xT_lo, x_hi, x_lo),
                                                          (ctx_raw[raw_of(b)], cT_hi, cT_lo, ctx_hi, ctx_lo)):
                        pool.wait_ge(rounded, b + 1)
                        nc.gpsimd.tensor_tensor(lo[:, b, :, :].rearrange("p k t -> p (k t)"), copied,
                                                hi[:, b, :, :].rearrange("p k t -> p (k t)").bitcast(F32),
                                                ALU.subtract).then_inc(done, 1)

                def split_w(g, part, par):
                    if part < KT:
                        wait(pool, wq_rounded, (g - 1) * KT + part + 1)
                        nc.gpsimd.tensor_tensor(wq_lo[par][:, part, :], wq_raw[:, part, :],
                                                wq_hi[par][:, part, :].bitcast(F32), ALU.subtract)
                        nc.gpsimd.tensor_tensor(wkv_lo[par][:, part, :], wkv_raw[:, part, :],
                                                wkv_hi[par][:, part, :].bitcast(F32),
                                                ALU.subtract).then_inc(wq_split, 1)
                    else:
                        h = part - KT
                        wait(pool, wo_rounded, g * HG + h + 1)
                        nc.gpsimd.tensor_tensor(wo_lo[par][:, h, :], wo_raw[:, h, :],
                                                wo_hi[par][:, h, :].bitcast(F32),
                                                ALU.subtract).then_inc(wo_split, 1)

                invert_std(0)
                invert_std(1)
                pool.wait_ge(wkv0_rounded, 1)
                nc.gpsimd.tensor_tensor(wkv_lo[0][:, :, :], wkv_raw[:], wkv_hi[0][:, :, :].bitcast(F32),
                                        ALU.subtract).then_inc(wkv0_split, 1)
                invert_std(2)

                def invert_std2(b):
                    pool.wait_ge(var2, b + 1)
                    nc.gpsimd.tensor_tensor(rstd[:, b, :], rstd[:, b, :], minus_half[:], ALU.pow).then_inc(rstd2, 1)

                def scale(pair, n):
                    m, par = pair * 2 + n, n % 2
                    wait(pool, centred, m + 1)
                    nc.gpsimd.tensor_tensor(w_full[:, par], w_full[:, par], scales[:, par, :, :], ALU.mult).then_inc(scaled, 1)

                def rest(pair, n):
                    m, par = pair * 2 + n, n % 2
                    wait(pool, w_rounded, m + 1)
                    nc.gpsimd.tensor_tensor(up_lo[:, par].rearrange("p k c -> p (k c)"), w_full[:, par, 0, :],
                                            up_hi[:, par].rearrange("p k c -> p (k c)").bitcast(F32), ALU.subtract)
                    nc.gpsimd.tensor_tensor(wd_lo[:, bass.ds(m * C, C)], w_full[:, par, 1, :],
                                            wd_hi[:, bass.ds(m * C, C)].bitcast(F32), ALU.subtract).then_inc(w_split, 1)

                def add_groups(pair, n, half):
                    m = pair * 2 + n
                    rows = LAST if isinstance(pair, int) and n == NT - 1 else P
                    wait(pool, odd_scaled, 4 * m + 2 * half + 2)
                    wait(pool, silu_done, 2 * m + half - 1)
                    nc.gpsimd.tensor_tensor(gate_sum[0:rows, half, :], later_sum[0:rows, 0, :], later_sum[0:rows, 1, :],
                                            ALU.add).then_inc(gate_summed, 1)

                def p_rest(j):
                    pool.wait_ge(p_rounded, j - 1)
                    nc.gpsimd.tensor_tensor(p_lo[:], probs[:, j % 2, :], p_hi[:].bitcast(F32),
                                            ALU.subtract).then_inc(p_split, 1)

                def add_share(s):
                    b = (s - 4) % B
                    pool.wait_ge(share_scaled, s - TAIL)
                    nc.gpsimd.tensor_tensor(acc[:, b, :], acc[:, b, :], share[:], ALU.add).then_inc(acc_done, 1)

                def apply_mask(j, s):
                    wait(pool, exp_done, j + 1)
                    pr = probs[:, s % 2, :].rearrange("p (h t) -> p h t", h=HG)
                    nc.gpsimd.tensor_tensor(pr, pr, keepT[:].unsqueeze(1).to_broadcast([P, HG, T]),
                                            ALU.mult).then_inc(masked, 1)

                def slot(base, group, s):
                    j = base + s
                    if s == SLOTS:
                        p_rest(s)
                    if TAIL < s < SLOTS + 2:
                        add_share(s)
                    if TAIL <= s < SLOTS:
                        p_rest(s)
                    if s == SLOTS:
                        apply_mask(s - 1, s - 1)
                    if runs(s - 3):
                        wait(pool, a_rounded, j - 2)
                        nc.gpsimd.tensor_tensor(aT_lo[:], attn[:], aT_hi[:].bitcast(F32),
                                                ALU.subtract).then_inc(a_split, 1)
                    if s == SLOTS + 2:
                        add_share(s)
                    if s == 0:
                        prep(1)
                    if s + 2 < B:
                        prep(s + 2)
                    if s >= B and runs(s + B):
                        split_w(group + s // B + 1, s % B, (s // B + 1) % 2)
                    if s >= DVE_ADDS and runs(s):
                        wait(pool, q_mul, j + 1)
                        wait(pool, tr_done, j)
                        nc.gpsimd.tensor_tensor(roped[:, 0:HG, :], q_cos[:], q_sin[:], ALU.add).then_inc(q_roped, 1)
                    if s == 1:
                        pool.wait_ge(tab_done, 1)
                    if runs(s - 1) and s != SLOTS:
                        apply_mask(j - 1, s - 1)
                    if s == SLOTS:
                        p_rest(s + 1)
                    if s + 3 < B:
                        invert_std(s + 3)
                    if s < B:
                        for head, part in early_parts[s]:
                            split_w(head, part, head)
                    if s >= TAIL + 4:
                        invert_std2(s - TAIL - 4)
                    if s == TAIL + 4:
                        scale(0, 0)
                    if s == TAIL + 6:
                        rest(0, 0)
                    if s == TAIL + 10:
                        add_groups(0, 0, 0)
                        invert_std2(7)
                        scale(0, 1)
                all_slots(pool, slot)

                def step(pair, n):
                    run = not isinstance(pair, int) or n < NT
                    if run and not (isinstance(pair, int) and n == 0):
                        add_groups(pair, n, 0)
                    if not isinstance(pair, int) or n + 1 < NT:
                        rest(pair, n + 1)
                    if run:
                        add_groups(pair, n, 1)
                    if not isinstance(pair, int) or n + 2 < NT:
                        scale(pair, n + 2)
                steps(pool, step)

            @block.scalar
            def _(act):
                def round_w(g, part, par):
                    if part < KT:
                        if part == 0:
                            wait(act, ld_wq, g * 16)
                            wait(act, ld_wkv, (g + 1) * 32)
                            wait(act, q_done, (g - 1) * B)
                            wait(act, kv_done, (g - 1) * B)
                        nc.scalar.copy(wq_hi[par][:, part, :], wq_raw[:, part, :])
                        nc.scalar.copy(wkv_hi[par][:, part, :], wkv_raw[:, part, :]).then_inc(wq_rounded, 1)
                    else:
                        h = part - KT
                        if h == 0:
                            wait(act, ld_wo, (g + 1) * 16)
                            wait(act, o_done, (g - 1) * B)
                        nc.scalar.copy(wo_hi[par][:, h, :], wo_raw[:, h, :]).then_inc(wo_rounded, 1)

                def prep_x(b):
                    act.wait_ge(x_T, b + 1)
                    if b > 0:
                        nc.scalar.copy(xn[:, 0, :], ps_x[:])
                    nc.scalar.copy(xT_hi[:, b, :, :].rearrange("p k t -> p (k t)"), ps_x[:]).then_inc(x_hi, 1)

                def prep_ctx(b):
                    act.wait_ge(ctx_T, b + 1)
                    if b > 0:
                        nc.scalar.copy(ctx_raw[raw_of(b)], ps_o[:])
                    nc.scalar.copy(cT_hi[:, b, :, :].rearrange("p k t -> p (k t)"), ps_o[:]).then_inc(ctx_hi, 1)

                def prep(b):
                    prep_x(b)
                    prep_ctx(b)

                prep_x(0)
                for k in range(KT):
                    act.wait_ge(ld_wq0[k // 2], 16)
                    nc.scalar.copy(wq_hi[0][:, k, :], wq_raw[:, k, :]).then_inc(wq0_rounded, 1)
                prep_ctx(0)
                act.wait_ge(ld_wkv, 32)
                nc.scalar.copy(wkv_hi[0][:, :, :], wkv_raw[:]).then_inc(wkv0_rounded, 1)
                act.wait_ge(ld_gates, 32)
                nc.scalar.activation(tgates[:], gates[:], ACT.Tanh).then_inc(tg_done, 1)

                def round_ffn(pair, n):
                    m, par = pair * 2 + n, n % 2
                    wait(act, odd_scaled, 4 * (m - 1))
                    nc.scalar.copy(gate_s32[:, par, :], gate_s16[:, bass.ds(m, 1), :].rearrange("p m k -> p (m k)")
                                   ).then_inc(gate_s_done, 1)
                    wait(act, scaled, m + 1)
                    wait(act, up_done, 2 * (m - 1))
                    nc.scalar.copy(up_hi[:, par].rearrange("p k c -> p (k c)"), w_full[:, par, 0, :])
                    nc.scalar.copy(wd_hi[:, bass.ds(m * C, C)], w_full[:, par, 1, :]).then_inc(w_rounded, 1)

                def scale_even(pair, n, half, k):
                    m = pair * 2 + n
                    rows = LAST if isinstance(pair, int) and n == NT - 1 else P
                    wait(act, gate_s_done, m + 1)
                    wait(act, group_done, 8 * m + 4 * half + k + 1)
                    wait(act, odd_scaled, 4 * m + 2 * half + k // 2 - 1)
                    nc.scalar.activation(first_sum[0:rows, k // 2, :], ps_g[0][0:rows, :], ACT.Copy,
                                         scale=gate_s32[0:rows, n % 2, k:k + 1]).then_inc(even_scaled, 1)

                def norm2_hi(b):
                    act.wait_ge(prep2_T, b + 1)
                    nc.scalar.copy(xT_hi[:, b, :, :].rearrange("p k t -> p (k t)"), norm2_bank(b)).then_inc(prep2_hi, 1)

                def round_qk(j, s):
                    wait(act, tr_done, j + 1)
                    wait(act, s_done, j)
                    nc.scalar.copy(qT_hi[:], ps_qT[:])
                    nc.scalar.copy(kT_hi[:], kv_bank(s)[:, 2, :]).then_inc(qk_rounded, 1)

                def round_p(j, s):
                    wait(act, masked, j + 1)
                    wait(act, pv_done, j)
                    nc.scalar.copy(p_hi[:], probs[:, s % 2, :]).then_inc(p_rounded, 1)

                def cap_and_exp(j, s):
                    wait(act, s_done, j + 1)
                    nc.scalar.activation(capped[:], ps_s[:], ACT.Tanh, scale=ATTN_MULT / MAX_ATTN).then_inc(tanh_done, 1)
                    wait(act, tanh_done, j + 1)
                    wait(act, p_split, j - 1)
                    nc.scalar.activation(probs[:, s % 2, :], capped[:], ACT.Exp,
                                         scale=MAX_ATTN).then_inc(exp_done, 1)

                def scale_share(s):
                    act.wait_ge(o_done, s - 3)
                    act.wait_ge(acc_done, s - 4)
                    act.wait_ge(kv_done, TAIL)
                    nc.scalar.activation(share[:], ps_o[:], ACT.Copy, scale=tgates[:, 0:1]).then_inc(share_scaled, 1)

                def slot(base, group, s):
                    j = base + s
                    if TAIL < s < SLOTS + 3 and s not in (SLOTS, SLOTS + 2):
                        scale_share(s)
                    if runs(s - 1) and s != SLOTS:
                        round_qk(j - 1, s - 1)
                    if runs(s - 2) and s != SLOTS + 1:
                        round_p(j - 2, s - 2)
                    if s == SLOTS:
                        scale_share(s)
                        cap_and_exp(s - 1, s - 1)
                    if runs(s - 3):
                        wait(act, norm_done, j - 2)
                        wait(act, o_done, j - 3)
                        nc.scalar.copy(aT_hi[:], attn[:]).then_inc(a_rounded, 1)
                    if s == SLOTS + 2:
                        scale_share(s)
                    if s < B:
                        for head, part in early_parts[s]:
                            round_w(head, part, head)
                    if s >= B and runs(s + B):
                        round_w(group + s // B + 1, s % B, (s // B + 1) % 2)
                    if s == 0:
                        prep(1)
                    if runs(s):
                        wait(act, kv_done, j + 1)
                        wait(act, pv_done, j - 3)
                        nc.scalar.copy(v_hi[:, s % 4, :], kv_bank(s)[:, 1, :]).then_inc(v_rounded, 1)
                    if s + 2 < B:
                        prep(s + 2)
                    if runs(s - 1) and s != SLOTS:
                        cap_and_exp(j - 1, s - 1)
                    if s == SLOTS:
                        round_p(s - 1, s - 1)
                    if s == TAIL + 9:
                        scale_even(0, 0, 0, 0)
                    if s == TAIL + 10:
                        scale_even(0, 0, 0, 2)
                    if s >= TAIL + 5:
                        norm2_hi(s - TAIL - 5)
                    if s == SLOTS - 1:
                        round_qk(s, s)
                    if s == TAIL + 5:
                        act.wait_ge(ld_gate_s, 16)
                        act.wait_ge(o_done, TAIL)
                        act.wait_ge(kv_done, TAIL + 1)
                        round_ffn(0, 0)
                    if s == TAIL + 10:
                        nc.scalar.activation(table_load[:], gates[:, 0:1], ACT.Silu)
                        norm2_hi(6)
                all_slots(act, slot)
                norm2_hi(7)

                def round_inner(pair, n, half):
                    m = pair * 2 + n
                    rows = LAST if isinstance(pair, int) and n == NT - 1 else P
                    wait(act, inner_done, 2 * m + half + 1)
                    if half == 0:
                        wait(act, first_down, m - 1)
                        dst = h_hi[0:rows, n % 2, :]
                    else:
                        dst = k_hi[0:rows, bass.ds(m * C, C)]
                    nc.scalar.copy(dst, inner[0:rows, half, :]).then_inc(inner_rounded, 1)

                def make_silu(pair, n, half):
                    m = pair * 2 + n
                    rows = LAST if isinstance(pair, int) and n == NT - 1 else P
                    wait(act, gate_summed, 2 * m + half + 1)
                    wait(act, inner_done, 2 * m + half - 1)
                    nc.scalar.activation(silu[0:rows, half, :], gate_sum[0:rows, half, :], ACT.Silu).then_inc(silu_done, 1)

                def step(pair, n):
                    first = isinstance(pair, int) and n == 0
                    run = not isinstance(pair, int) or n < NT
                    second = isinstance(pair, int) and n == 1
                    if run and not first and not second:
                        scale_even(pair, n, 0, 0)
                    if not first:
                        round_inner(pair, n - 1, 1)
                    if run and not first:
                        scale_even(pair, n, 0, 2)
                    if first or second:
                        scale_even(pair, n, 1, 0)
                    if not isinstance(pair, int) or n + 1 < NT:
                        round_ffn(pair, n + 1)
                    if run and not first and not second:
                        scale_even(pair, n, 1, 0)
                    if run:
                        make_silu(pair, n, 0)
                        scale_even(pair, n, 1, 2)
                        round_inner(pair, n, 0)
                        if first:
                            scale_even(pair, 1, 0, 0)
                        make_silu(pair, n, 1)
                steps(act, step)
                for b in range(B):
                    act.wait_ge(down_done, b + 1)
                    wait(act, sum_done, b - 1)
                    nc.scalar.copy(y16[:, b % 2, :], ps_d[b % 4][:]).then_inc(y_done, 1)

            @block.vector
            def _(dve):
                def norm_moments(b):
                    dve.wait_ge(ld_x[b], 16)
                    nc.vector.bn_stats(stats[:, b, :], acc[:, b, :]).then_inc(stats_done, 1)
                    dve.wait_ge(stats_done, b + 1)
                    nc.vector.bn_aggr(moments[:, b, :], stats[:, b, :]).then_inc(moments_done, 1)
                    dve.wait_ge(moments_done, b + 1)
                    nc.vector.tensor_scalar(rstd[:, b, :], moments[:, b, 1:2], EPS, None, ALU.add).then_inc(var_done, 1)

                def norm_apply(b):
                    dve.wait_ge(rstd_done, b + 1)
                    wait(dve, x_lo, b)
                    nc.vector.tensor_scalar(xn[:, 0, :], acc[:, b, :], moments[:, b, 0:1], rstd[:, b, :],
                                            ALU.subtract, ALU.mult).then_inc(xn_done, 1)

                norm_moments(0)
                norm_apply(0)
                dve.wait_ge(ld_mask, 16)
                nc.vector.tensor_copy(mask_f[:], mask_bytes[:].bitcast(U8)).then_inc(mask_step, 1)
                dve.wait_ge(mask_step, 1)
                nc.vector.reduce_sum(seen[:], mask_f[:], AX_X).then_inc(mask_step, 1)
                dve.wait_ge(mask_step, 2)
                nc.vector.tensor_scalar(live[:], seen[:], 1.0, None, ALU.min).then_inc(mask_step, 1)
                dve.wait_ge(mask_step, 3)
                nc.vector.tensor_scalar(dead[:], live[:], -1.0, 1.0, ALU.mult, ALU.add).then_inc(mask_step, 1)
                dve.wait_ge(mask_step, 4)
                nc.vector.tensor_scalar(keep[:], mask_f[:], dead[:], None, ALU.max).then_inc(mask_step, 1)
                def prep_rest(bank, hi, lo, rounded, done):
                    dve.wait_ge(rounded, 1)
                    nc.vector.tensor_tensor(lo[:, 0, :, :].rearrange("p k t -> p (k t)"), bank[:],
                                            hi[:, 0, :, :].rearrange("p k t -> p (k t)").bitcast(F32),
                                            ALU.subtract).then_inc(done, 1)

                prep_rest(ps_x, xT_hi, xT_lo, x_hi, x_lo)
                for k in range(KT):
                    dve.wait_ge(wq0_rounded, k + 1)
                    nc.vector.tensor_tensor(wq_lo[0][:, k, :], wq_raw[:, k, :], wq_hi[0][:, k, :].bitcast(F32),
                                            ALU.subtract).then_inc(wq0_split, 1)
                prep_rest(ps_o, cT_hi, cT_lo, ctx_hi, ctx_lo)
                dve.wait_ge(ld_tab, 16)
                nc.vector.tensor_scalar(q_tab[:], cs_tab[:], live[:], None, ALU.mult).then_inc(mask_step, 1)
                norm_moments(1)
                norm_apply(1)
                norm_moments(2)
                dve.wait_ge(keep_T, 1)
                nc.vector.tensor_copy(keepT[:], ps_pv[:, 0:T]).then_inc(tab_done, 1)
                dve.wait_ge(mask_step, 6)
                dve.wait_ge(tg_done, 1)

                def rope_products(xs, cs, sn, tab, mul):
                    heads = xs.shape[1]
                    def t(i, lo, hi):
                        return tab[:, i, lo:hi].unsqueeze(1).to_broadcast([P, heads, hi - lo])
                    h = D // 2
                    nc.vector.tensor_tensor(cs, xs, t(0, 0, D), ALU.mult)
                    nc.vector.tensor_tensor(sn[:, :, 0:h], xs[:, :, h:D], t(1, 0, h), ALU.mult)
                    nc.vector.tensor_tensor(sn[:, :, h:D], xs[:, :, 0:h], t(1, h, D), ALU.mult).then_inc(mul, 1)

                def unpack(pair, n, parts=range(4)):
                    m, par = pair * 2 + n, n % 2
                    q = packed[:, par].rearrange("p i c -> p (i c)")
                    if 0 in parts:
                        wait(dve, ld_q[par], (pair + n // 2 + 1) * (Q_LOADS * 16))
                        nc.vector.tensor_scalar(q, q, nib[:, 0:1], 15, ALU.logical_shift_right,
                                                ALU.bitwise_and).then_inc(unpacked, 1)
                    if 1 in parts:
                        zx = zero_x[:].rearrange("p (w e) -> p w e", e=PACK)
                        wait(dve, ld_zs[par], (pair + n // 2 + 1) * (ZS_LOADS * 16))
                        wait(dve, centred, m)
                        nc.vector.tensor_tensor(zx, zeros[:, par, :].unsqueeze(2).to_broadcast([P, 3 * WORDS, PACK]),
                                                nib[:, 1:1 + PACK].unsqueeze(1).to_broadcast([P, 3 * WORDS, PACK]),
                                                ALU.logical_shift_right).then_inc(zero_shifted, 1)
                    if 2 in parts:
                        wait(dve, zero_shifted, m + 1)
                        nc.vector.tensor_scalar(zero_x[:], zero_x[:], 15, None, ALU.bitwise_and).then_inc(zero_ready, 1)
                    if 3 in parts:
                        wait(dve, zero_ready, m + 1)
                        wait(dve, w_split, m - 1)
                        wait(dve, up_done, 2 * (m - 1))
                        nc.vector.scalar_tensor_tensor(out=gate_int[:, par].rearrange("p k c -> p (k c)"), in0=q[:, 0:C],
                                                       scalar=1.0, in1=zero_x[:, 0:C], op0=ALU.subtract,
                                                       op1=ALU.subtract).then_inc(gate_centred, 1)
                        nc.vector.scalar_tensor_tensor(out=w_full[:, par].rearrange("p i c -> p (i c)"), in0=q[:, C:3 * C],
                                                       scalar=1.0, in1=zero_x[:, C:3 * C], op0=ALU.subtract,
                                                       op1=ALU.subtract).then_inc(centred, 1)

                def scale_odd(pair, n, half, k):
                    m = pair * 2 + n
                    rows = LAST if isinstance(pair, int) and n == NT - 1 else P
                    wait(dve, group_done, 8 * m + 4 * half + k + 1)
                    wait(dve, even_scaled, 4 * m + 2 * half + k // 2 + 1)
                    wait(dve, gate_summed, 2 * m + half)
                    nc.vector.scalar_tensor_tensor(out=later_sum[0:rows, k // 2, :], in0=ps_g[1][0:rows, :],
                                                   scalar=gate_s32[0:rows, n % 2, k:k + 1],
                                                   in1=first_sum[0:rows, k // 2, :], op0=ALU.mult,
                                                   op1=ALU.add).then_inc(odd_scaled, 1)

                def moments2_of(b):
                    dve.wait_ge(acc_done, TAIL + b + 1)
                    nc.vector.bn_stats(stats[:, b, :], acc[:, b, :]).then_inc(stats2, 1)
                    dve.wait_ge(stats2, b + 1)
                    nc.vector.bn_aggr(moments[:, b, :], stats[:, b, :]).then_inc(moments2, 1)
                    dve.wait_ge(moments2, b + 1)
                    nc.vector.tensor_scalar(rstd[:, b, :], moments[:, b, 1:2], EPS, None, ALU.add).then_inc(var2, 1)

                def norm2_apply(b):
                    dve.wait_ge(rstd2, b + 1)
                    wait(dve, prep2_T, b - 1)
                    nc.vector.tensor_scalar(xn[:, b % 2, :], acc[:, b, :], moments[:, b, 0:1], rstd[:, b, :],
                                            ALU.subtract, ALU.mult).then_inc(xn2, 1)

                def norm2_lo(b):
                    dve.wait_ge(prep2_hi, b + 1)
                    nc.vector.tensor_tensor(xT_lo[:, b, :, :].rearrange("p k t -> p (k t)"), norm2_bank(b),
                                            xT_hi[:, b, :, :].rearrange("p k t -> p (k t)").bitcast(F32),
                                            ALU.subtract).then_inc(prep2_lo, 1)

                def split_qk(j, s):
                    wait(dve, qk_rounded, j + 1)
                    nc.vector.tensor_tensor(qT_lo[:], ps_qT[:], qT_hi[:].bitcast(F32), ALU.subtract)
                    nc.vector.tensor_tensor(kT_lo[:], kv_bank(s)[:, 2, :], kT_hi[:].bitcast(F32),
                                            ALU.subtract).then_inc(qk_split, 1)

                def slot(base, group, s):
                    j = base + s
                    if runs(s - 1) and s != SLOTS:
                        split_qk(j - 1, s - 1)
                    if 1 <= s < B - 2:
                        norm_apply(s + 2)
                    if s >= TAIL + 5:
                        norm2_apply(s - TAIL - 5)
                    if TAIL + 6 <= s < TAIL + 10:
                        norm2_lo(s - TAIL - 6)
                    if s == TAIL + 10:
                        scale_odd(0, 0, 0, 3)
                    if runs(s - 2) and s < TAIL:
                        par = (s - 2) % 2
                        wait(dve, p_rounded, j - 1)
                        nc.vector.tensor_tensor(p_lo[:], probs[:, par, :], p_hi[:].bitcast(F32),
                                                ALU.subtract).then_inc(p_split, 1)
                    if runs(s):
                        wait(dve, q_done, j + 1)
                        wait(dve, q_roped, j)
                        rope_products(ps_q, q_cos[:], q_sin[:], q_tab, q_mul)
                        if s < DVE_ADDS:
                            dve.wait_ge(q_mul, s + 1)
                            wait(dve, tr_done, s)
                            nc.vector.tensor_tensor(roped[:, 0:HG, :], q_cos[:], q_sin[:], ALU.add).then_inc(q_roped, 1)
                        if s == 0:
                            norm_apply(2)
                        wait(dve, v_rounded, j + 1)
                        nc.vector.tensor_tensor(v_lo[:, s % 4, :], kv_bank(s)[:, 1, :], v_hi[:, s % 4, :].bitcast(F32),
                                                ALU.subtract).then_inc(v_split, 1)
                        rope_products(kv_bank(s)[:, 0:1, :], k_cos[:].unsqueeze(1), k_sin[:].unsqueeze(1), cs_tab, k_mul)
                        wait(dve, k_mul, j + 1)
                        wait(dve, tr_done, j)
                        nc.vector.tensor_tensor(roped[:, HG, :], k_cos[:], k_sin[:], ALU.add).then_inc(k_roped, 1)
                    if s == TAIL + 10:
                        norm2_lo(5)
                    if s >= TAIL + 4 and s != TAIL + 9:
                        moments2_of(s - TAIL - 4)
                    if s == TAIL + 10:
                        norm2_apply(6)
                    if s == SLOTS - 1:
                        split_qk(s, s)
                    if runs(s - 2):
                        wait(dve, tot_done, j - 1)
                        wait(dve, norm_done, j - 2)
                        nc.vector.reciprocal(r_tot[:], ps_tot[:]).then_inc(inverted, 1)
                        wait(dve, inverted, j - 1)
                        wait(dve, pv_done, j - 1)
                        wait(dve, a_split, j - 2)
                        nc.vector.tensor_tensor(attn[:], ps_pv[:], r_tot[:], ALU.mult).then_inc(norm_done, 1)
                    if s == TAIL + 9:
                        scale_odd(0, 0, 0, 1)
                        moments2_of(5)
                        norm2_lo(4)
                    if s == TAIL:
                        dve.wait_ge(ld_nib, 16)
                        unpack(0, 0, (0,))
                        unpack(0, 1, (0,))
                        dve.wait_ge(q_done, TAIL)
                        dve.wait_ge(kv_done, TAIL)
                    if s == TAIL + 3:
                        dve.wait_ge(o_done, TAIL)
                    if TAIL + 1 <= s < TAIL + 4:
                        unpack(0, 0, (s - TAIL,))
                    if TAIL + 4 <= s < TAIL + 6:
                        unpack(0, 1, (s - TAIL - 3,))
                    if runs(s - 3) and not TAIL <= s < SLOTS + 2:
                        b = (s - 3) % B
                        wait(dve, o_done, j - 2)
                        wait(dve, acc_done, j - 3)
                        nc.vector.scalar_tensor_tensor(out=acc[:, b, :], in0=ps_o[:], scalar=tgates[:, 0:1],
                                                       in1=acc[:, b, :], op0=ALU.mult,
                                                       op1=ALU.add).then_inc(acc_done, 1)
                    if s + 3 < B:
                        norm_moments(s + 3)
                    if s == TAIL + 10:
                        moments2_of(7)
                        norm2_lo(6)
                all_slots(dve, slot)
                norm2_apply(7)
                unpack(0, 1, (3,))
                norm2_lo(7)

                def make_inner(pair, n, half):
                    m = pair * 2 + n
                    rows = LAST if isinstance(pair, int) and n == NT - 1 else P
                    wait(dve, silu_done, 2 * m + half + 1)
                    wait(dve, up_done, 2 * m + half + 1)
                    wait(dve, inner_split, 2 * m + half - 1)
                    nc.vector.tensor_tensor(inner[0:rows, half, :], ps_u[half][0:rows, :], silu[0:rows, half, :],
                                            ALU.mult).then_inc(inner_done, 1)

                def inner_rest(pair, n, half):
                    m = pair * 2 + n
                    rows = LAST if isinstance(pair, int) and n == NT - 1 else P
                    wait(dve, inner_rounded, 2 * m + half + 1)
                    if half == 0:
                        lo, hi = h_lo[0:rows, n % 2, :], h_hi[0:rows, n % 2, :]
                    else:
                        lo, hi = k_lo[0:rows, bass.ds(m * C, C)], k_hi[0:rows, bass.ds(m * C, C)]
                    nc.vector.tensor_tensor(lo, inner[0:rows, half, :], hi.bitcast(F32),
                                            ALU.subtract).then_inc(inner_split, 1)

                def step(pair, n):
                    first = isinstance(pair, int) and n == 0
                    run = not isinstance(pair, int) or n < NT
                    ahead = not isinstance(pair, int) or n + 2 < NT
                    second = isinstance(pair, int) and n == 1
                    if run and not first and not second:
                        scale_odd(pair, n, 0, 1)
                    if second:
                        scale_odd(pair, n, 0, 3)
                    if ahead:
                        unpack(pair, n + 2, (0,))
                    if not first:
                        inner_rest(pair, n - 1, 1)
                    if run and not first and not second:
                        scale_odd(pair, n, 0, 3)
                    if ahead:
                        unpack(pair, n + 2, (1,))
                    if run:
                        scale_odd(pair, n, 1, 1)
                        make_inner(pair, n, 0)
                        scale_odd(pair, n, 1, 3)
                        inner_rest(pair, n, 0)
                    if ahead and first:
                        unpack(pair, n + 2, (2,))
                        scale_odd(pair, 1, 0, 1)
                    elif ahead:
                        unpack(pair, n + 2, (2, 3))
                    if run:
                        make_inner(pair, n, 1)
                    if first:
                        unpack(pair, n + 2, (3,))
                steps(dve, step)
                for b in range(B):
                    dve.wait_ge(y_done, b + 1)
                    nc.vector.scalar_tensor_tensor(out=acc[:, b, :], in0=y16[:, b % 2, :], scalar=tgates[:, 1:2],
                                                   in1=acc[:, b, :], op0=ALU.mult, op1=ALU.add).then_inc(sum_done, 1)

            @block.tensor
            def _(pe):
                pe.wait_ge(id_done, 1)

                def prep(b):
                    pe.wait_ge(xn_done, b + 1)
                    wait(pe, x_lo, b)
                    for i in range(KT):
                        mm = nc.tensor.transpose(ps_x[:, i * T:(i + 1) * T], xn[:, 0, i * P:(i + 1) * P], ident[:])
                    mm.then_inc(x_T, 1)
                    i = raw_of(b)
                    pe.wait_ge(ld_ctx[i], 16 if b < 2 else b // 2 * 16)
                    wait(pe, ctx_lo, b)
                    wait(pe, acc_done, b - 5)
                    for k in range(KT):
                        mm = nc.tensor.transpose(ps_o[:, k * T:(k + 1) * T], ctx_raw[i][:, k * P:(k + 1) * P], ident[:])
                    mm.then_inc(ctx_T, 1)

                prep(0)
                pe.wait_ge(mask_step, 5)
                nc.tensor.transpose(ps_pv[:, 0:T], keep[:], ident[:]).then_inc(keep_T, 1)

                def gate_up(pair, n, half, groups=range(KT)):
                    m, par = pair * 2 + n, n % 2
                    cols = LAST if isinstance(pair, int) and n == NT - 1 else P
                    seqs = slice(half * HALF, (half + 1) * HALF)
                    for k in groups:
                        wait(pe, (even_scaled, odd_scaled)[k % 2], 4 * m + 2 * half + k // 2)
                        bank = ps_g[k % 2][0:cols, :].rearrange("p (b t) -> p b t", b=HALF)
                        w = gate_int[:, par, k, 0:cols]
                        nc.tensor.matmul(bank, w, xT_hi[:, seqs, k, :], start=True, stop=False)
                        nc.tensor.matmul(bank, w, xT_lo[:, seqs, k, :], start=False, stop=True).then_inc(group_done, 1)
                        if k == 0:
                            wait(pe, inner_done, 2 * m + half - 1)
                        mm = split_matmul(nc, ps_u[half][0:cols, :].rearrange("p (b t) -> p b t", b=HALF),
                                          up_hi[:, par, k, 0:cols], up_lo[:, par, k, 0:cols],
                                          xT_hi[:, seqs, k, :], xT_lo[:, seqs, k, :], k == 0, k == KT - 1)
                        if k == KT - 1:
                            mm.then_inc(up_done, 1)

                def step(pair, n):
                    wait(pe, gate_centred, pair * 2 + n + 1)
                    wait(pe, w_split, pair * 2 + n + 1)
                    for half in range(2):
                        gate_up(pair, n, half)

                def norm2_T(b):
                    pe.wait_ge(xn2, b + 1)
                    if b < B - 2:
                        wait(pe, prep2_lo, b)
                    for i in range(KT):
                        mm = nc.tensor.transpose(norm2_bank(b)[:, i * T:(i + 1) * T], xn[:, b % 2, i * P:(i + 1) * P], ident[:])
                    mm.then_inc(prep2_T, 1)

                def down_first(pair, n, start):
                    m, par = pair * 2 + n, n % 2
                    rows = LAST if isinstance(pair, int) and n == NT - 1 else P
                    last = isinstance(pair, int) and n == NT - 1
                    wait(pe, inner_split, 2 * m + 1)
                    for b in range(HALF):
                        mm = split_matmul(nc, ps_d[b][:], h_hi[0:rows, par, b * T:(b + 1) * T],
                                          h_lo[0:rows, par, b * T:(b + 1) * T],
                                          wd_hi[0:rows, bass.ds(m * C, C)], wd_lo[0:rows, bass.ds(m * C, C)], start, last)
                        if last:
                            mm.then_inc(down_done, 1)
                    return mm

                pe.wait_ge(ones_done, 1)

                def transpose_qk(j, s):
                    wait(pe, q_roped, j + 1)
                    wait(pe, k_roped, j + 1)
                    wait(pe, qk_split, j)
                    wait(pe, v_split, j + 1)
                    for h in range(HG):
                        nc.tensor.transpose(ps_qT[:, h * T:(h + 1) * T], roped[:, h, :], ident[:])
                    nc.tensor.transpose(kv_bank(s)[:, 2, :], roped[:, HG, :], ident[:]).then_inc(tr_done, 1)

                def slot(base, group, s):
                    j = base + s
                    g = group + s // B
                    wpar = (s // B) % 2
                    if runs(s - 1) and s != SLOTS:
                        transpose_qk(j - 1, s - 1)
                    if runs(s):
                        b = s % B
                        if s < B:
                            pe.wait_ge(x_lo, b + 1)
                        elif b == 0:
                            wait(pe, wq_split, g * KT)
                        for k in range(KT):
                            if s == 0:
                                pe.wait_ge(wq0_split, k + 1)
                            mm = split_matmul(nc, ps_q[:].rearrange("p h d -> p (h d)"),
                                              xT_hi[:, b, k, :], xT_lo[:, b, k, :],
                                              wq_hi[wpar][:, k, :], wq_lo[wpar][:, k, :], k == 0, k == KT - 1)
                        mm.then_inc(q_done, 1)
                        if s == 0:
                            prep(1)
                            pe.wait_ge(wkv0_split, 1)
                        if s < B:
                            pe.wait_ge(ctx_lo, b + 1)
                        if kv_bank(s) is kv_bank(s - 1):
                            wait(pe, qk_split, j)
                        for k in range(KT):
                            mm = split_matmul(nc, kv_bank(s)[:, 0:2, :].rearrange("p h d -> p (h d)"),
                                              cT_hi[:, b, k, :], cT_lo[:, b, k, :],
                                              wkv_hi[wpar][:, k, :], wkv_lo[wpar][:, k, :], k == 0, k == KT - 1)
                        mm.then_inc(kv_done, 1)
                        if s + 2 < B:
                            prep(s + 2)
                    if runs(s - 1):
                        wait(pe, qk_split, j)
                        wait(pe, tanh_done, j - 1)
                        split_matmul(nc, ps_s[:], kT_hi[:], kT_lo[:],
                                     qT_hi[:], qT_lo[:], True, True).then_inc(s_done, 1)
                    if runs(s - 2):
                        vb = (s - 2) % 4
                        wait(pe, p_split, j - 1)
                        wait(pe, norm_done, j - 2)
                        if s == 2:
                            pe.wait_ge(tab_done, 1)
                        nc.tensor.matmul(ps_tot[:], ones[:], p_hi[:], start=True, stop=False)
                        nc.tensor.matmul(ps_tot[:], ones[:], p_lo[:], start=False, stop=True).then_inc(tot_done, 1)
                        mm = split_matmul(nc, ps_pv[:], v_hi[:, vb, :], v_lo[:, vb, :], p_hi[:], p_lo[:], True, True)
                        mm.then_inc(pv_done, 1)
                    if s == TAIL + 9:
                        pe.wait_ge(gate_centred, 1)
                        pe.wait_ge(w_split, 1)
                        pe.wait_ge(prep2_lo, HALF)
                        pe.wait_ge(q_roped, SLOTS)
                        pe.wait_ge(qk_split, SLOTS)
                        gate_up(0, 0, 0, (0, 1))
                    if s == TAIL + 10:
                        gate_up(0, 0, 0, (2, 3))
                    if s >= TAIL + 5:
                        norm2_T(s - TAIL - 5)
                    if s == SLOTS - 1:
                        transpose_qk(s, s)
                    if runs(s - 3):
                        wp = ((s - 3) // B) % 2
                        if (s - 3) % B == 0:
                            wait(pe, wo_split, (group + (s - 3) // B + 1) * HG)
                        wait(pe, a_split, j - 2)
                        wait(pe, acc_done, j - 3)
                        if s < B:
                            pe.wait_ge(ctx_hi, min(s + 3, B))
                        for h in range(HG):
                            mm = split_matmul(nc, ps_o[:], aT_hi[:, h * T:(h + 1) * T],
                                              aT_lo[:, h * T:(h + 1) * T],
                                              wo_hi[wp][:, h, :], wo_lo[wp][:, h, :], h == 0, h == HG - 1)
                        mm.then_inc(o_done, 1)
                    if s == TAIL + 10:
                        pe.wait_ge(norm_done, SLOTS)
                        norm2_T(6)
                all_slots(pe, slot)
                norm2_T(7)
                pe.wait_ge(prep2_lo, B)
                gate_up(0, 0, 1)
                step(0, 1)
                down_first(0, 0, True).then_inc(first_down, 1)
                with pe.Fori(0, 4) as i:
                    for n in range(2):
                        step(i, n + 2)
                        down_first(i, n + 1, False).then_inc(first_down, 1)
                step(0, NT - 1)
                down_first(0, NT - 2, False).then_inc(first_down, 1)
                down_first(0, NT - 1, False)
                for b in range(HALF, B):
                    pe.wait_ge(inner_split, 2 * NT)
                    pe.wait_ge(y_done, b - HALF + 1)
                    for n in range(NT):
                        rows = LAST if n == NT - 1 else P
                        at = n * C + (b - HALF) * T
                        mm = split_matmul(nc, ps_d[b % 4][:], k_hi[0:rows, at:at + T], k_lo[0:rows, at:at + T],
                                          wd_hi[0:rows, n * C:(n + 1) * C], wd_lo[0:rows, n * C:(n + 1) * C],
                                          n == 0, n == NT - 1)
                    mm.then_inc(down_done, 1)


_OUT = ((B, T, C), "float32")


def rope_tables():
    exponents = np.arange(0, D, 2, dtype=np.float32)
    inv_freq = (np.float32(1.0) / np.float32(10000.0) ** (exponents / np.float32(D))).astype(np.float32)
    phase = np.arange(T, dtype=np.float32)[:, None] * inv_freq[None, :]
    phase = np.concatenate([phase, phase], axis=1).astype(np.float32)
    sign = np.where(np.arange(D) < D // 2, -1.0, 1.0).astype(np.float32)
    return np.stack([np.cos(phase), np.sin(phase) * sign], axis=1).astype(np.float32)


def nibble_table():
    rows = np.arange(P)[:, None] % PACK * 4
    return np.concatenate([rows, np.tile(np.arange(PACK) * 4, (P, 1))], axis=1).astype(np.uint32)


def kernel(x, ctx_4096, mask_1x1xSxS2_bk0, g_xattn, g_ffn, L0_xattn_Wq, L0_xattn_Wk, L0_xattn_Wv, L0_xattn_Wo,
           L0_ffn_gate_qweight, L0_ffn_gate_scales, L0_ffn_gate_zeros, L0_ffn_up_qweight, L0_ffn_up_scales,
           L0_ffn_up_zeros, L0_ffn_down_qweight, L0_ffn_down_scales, L0_ffn_down_zeros):
    import concourse.bacc as bacc
    from concourse.bass_utils import run_bass_kernel_spmd

    def by_column(a):
        a = np.asarray(a)
        padded = np.zeros((KT, NT * P), a.dtype)
        padded[:, :INTER] = a
        return np.ascontiguousarray(padded.reshape(KT, NT, P).transpose(2, 1, 0))

    def bits(a):
        return np.ascontiguousarray(a).view(np.uint32)

    ins = [("x", np.ascontiguousarray(x)), ("ctx", np.ascontiguousarray(ctx_4096)),
           ("mask", np.ascontiguousarray(mask_1x1xSxS2_bk0).reshape(T, T).view(np.uint32)),
           ("g_xattn", np.ascontiguousarray(g_xattn)), ("g_ffn", np.ascontiguousarray(g_ffn)),
           ("Wq", np.ascontiguousarray(L0_xattn_Wq)), ("Wk", np.ascontiguousarray(L0_xattn_Wk)),
           ("Wv", np.ascontiguousarray(L0_xattn_Wv)), ("Wo", np.ascontiguousarray(L0_xattn_Wo)),
           ("gate_q", bits(L0_ffn_gate_qweight)), ("gate_s", by_column(L0_ffn_gate_scales)),
           ("gate_z", bits(L0_ffn_gate_zeros)),
           ("up_q", bits(L0_ffn_up_qweight)), ("up_s", np.ascontiguousarray(L0_ffn_up_scales)),
           ("up_z", bits(L0_ffn_up_zeros)),
           ("down_q", bits(L0_ffn_down_qweight)), ("down_s", np.ascontiguousarray(L0_ffn_down_scales)),
           ("down_z", bits(L0_ffn_down_zeros)),
           ("cos_sin", rope_tables()), ("nibble", nibble_table())]
    nc = bacc.Bacc("TRN2", target_bir_lowering=False, num_devices=1, dynamic_dma_scratch_size=256)
    arrays, args = {}, []
    for name, a in ins:
        arrays[f"in_{name}"] = a
        args.append(nc.dram_tensor(f"in_{name}", a.shape, mybir.dt.from_np(a.dtype), kind="ExternalInput").ap())
    args.append(nc.dram_tensor("out_dram", _OUT[0], F32, kind="ExternalOutput").ap())
    flamingo_block(nc, *args)
    r = run_bass_kernel_spmd(nc, [arrays], core_ids=[0])
    return r.results[0]["out_dram"]
```
